# Optimizing a Trainium2 kernel written in Bass

```python
import numpy as np
import jax
import jax.numpy as jnp

def _softmax(x, axis=-1):
    return jax.nn.softmax(x, axis=axis)

def _gelu(x):
    return jax.nn.gelu(x, approximate=True)

def _silu(x):
    return jax.nn.silu(x)

def _sigmoid(x):
    return jax.nn.sigmoid(x)

def _layernorm(x, axis=-1, eps=1e-05):
    m = jnp.mean(x, axis=axis, keepdims=True)
    v = jnp.var(x, axis=axis, keepdims=True)
    return (x - m) / jnp.sqrt(v + eps)

def _scatter_add(tgt, idx, src, axis=0):
    return tgt.at[idx].add(src)

def _segment_sum(src, seg, n):
    return jax.ops.segment_sum(src, seg, n)
kernel_name = 'mk_cond_seq_d4_seqx_r2_bc113f'

def setup_inputs(seed: int=0):
    np.random.seed(seed)
    _w = jnp.asarray

    def _rec_inputs():
        import jax
        import jax.numpy as jnp
        _rk = jax.random.key(seed)
        x = -7.109e-05 + 0.9999 * jax.random.normal(jax.random.fold_in(_rk, 1), (8, 512, 512), jnp.float32)
        _lenS = 512 - jax.random.randint(jax.random.fold_in(_rk, 7), (8,), 0, max(1, 512 // 4) + 1, jnp.int32)
        _lenS2 = 512 - jax.random.randint(jax.random.fold_in(_rk, 8), (8,), 0, max(1, 512 // 4) + 1, jnp.int32)
        condB_theta = jax.random.uniform(jax.random.fold_in(_rk, 11), (8,), jnp.float32, 0.0, 0.983423)
        condB_phi = jax.random.uniform(jax.random.fold_in(_rk, 12), (8,), jnp.float32, 0.0, 0.961312)
        itok_B_34_63 = jax.random.randint(jax.random.fold_in(_rk, 14), (8,), 34, 64, jnp.int32)
        fside_Bx16xSxS_0 = -1.47943e-05 + 1.00017 * jax.random.normal(jax.random.fold_in(_rk, 15), (8, 16, 512, 512), jnp.float32)
        itok_B_0_15 = jax.random.randint(jax.random.fold_in(_rk, 16), (8,), 0, 16, jnp.int32)
        condB_dt = jax.random.uniform(jax.random.fold_in(_rk, 17), (8,), jnp.float32, 0.0, 0.981965)
        _validS = jnp.arange(512)[None, :] < _lenS[:, None]
        _validS2 = jnp.arange(512)[None, :] < _lenS2[:, None]
        _causal = jnp.tril(jnp.ones((512, 512), dtype=bool))
        mask_Bx1xSxS_bk0 = jnp.logical_not(jnp.broadcast_to(_validS[:, None, None, :], (8, 1, 512, 512)))
        return (x, condB_theta, condB_phi, itok_B_34_63, fside_Bx16xSxS_0, itok_B_0_15, condB_dt, mask_Bx1xSxS_bk0)
    x, condB_theta, condB_phi, itok_B_34_63, fside_Bx16xSxS_0, itok_B_0_15, condB_dt, mask_Bx1xSxS_bk0 = _rec_inputs()

    def _L0_cond_setup():
        import jax, jax.numpy as jnp
        import numpy as np
        key = jax.random.key(seed)
        k1, k2, k3 = jax.random.split(key, 3)
        B, N, D = (16, 2048, 512)
        embeddings = jax.random.normal(k1, (B, N, D), dtype=jnp.float32)
        theta = jax.random.uniform(k2, (B,), dtype=jnp.float32)
        phi = jax.random.uniform(k3, (B,), dtype=jnp.float32)
        return {'embeddings': embeddings, 'theta': theta, 'phi': phi}
    _L0_cond_all = _L0_cond_setup()
    _L0_cond_in = {k: v for k, v in _L0_cond_all.items() if k in ()}
    del _L0_cond_all

    def _L1_cond_setup():
        import jax, jax.numpy as jnp
        import numpy as np
        import math
        D_MODEL = 512
        N_HEAD = 16
        HEAD_DIM = D_MODEL // N_HEAD
        D_FF = 2048
        NUM_STEPS = 100.0
        RESCALE = 4000.0
        EPS = 1e-05

        def _sin_emb(t):
            half = D_MODEL // 2
            x = t.astype(jnp.float32) / NUM_STEPS * RESCALE
            freqs = jnp.exp(jnp.arange(half, dtype=jnp.float32) * (-math.log(10000.0) / (half - 1)))
            e = x[:, None] * freqs[None, :]
            return jnp.concatenate([jnp.sin(e), jnp.cos(e)], axis=-1)

        def _ln(x):
            m = jnp.mean(x, axis=-1, keepdims=True)
            v = jnp.var(x, axis=-1, keepdims=True)
            return (x - m) / jnp.sqrt(v + EPS)

        def _gelu2(x):
            return x * jax.nn.sigmoid(1.702 * x)
        key = jax.random.key(seed)
        ks = jax.random.split(key, 24)
        B, S, D, F = (4, 256, D_MODEL, D_FF)
        std = 0.02
        inp = {'src': jax.random.normal(ks[0], (B, S, D), dtype=jnp.float32), 'src_mask': jax.random.randint(ks[1], (B, 1, S, S), 0, 2).astype(bool), 'timestep': jax.random.randint(ks[2], (B,), 0, 100, dtype=jnp.int32), 'attention_bias': jax.random.normal(ks[3], (B, N_HEAD, S, S), dtype=jnp.float32), 'W_ada': jax.random.normal(ks[4], (D, 2 * D), dtype=jnp.float32) * std, 'b_ada': jnp.zeros((2 * D,), dtype=jnp.float32), 'Wq': jax.random.normal(ks[5], (D, D), dtype=jnp.float32) * std, 'bq': jnp.zeros((D,), dtype=jnp.float32), 'Wk': jax.random.normal(ks[6], (D, D), dtype=jnp.float32) * std, 'bk': jnp.zeros((D,), dtype=jnp.float32), 'Wv': jax.random.normal(ks[7], (D, D), dtype=jnp.float32) * std, 'bv': jnp.zeros((D,), dtype=jnp.float32), 'Wo': jax.random.normal(ks[8], (D, D), dtype=jnp.float32) * std, 'bo': jnp.zeros((D,), dtype=jnp.float32), 'W1': jax.random.normal(ks[9], (D, F), dtype=jnp.float32) * std, 'b1': jnp.zeros((F,), dtype=jnp.float32), 'W2': jax.random.normal(ks[10], (F, D), dtype=jnp.float32) * std, 'b2': jnp.zeros((D,), dtype=jnp.float32), 'g2': jnp.ones((D,), dtype=jnp.float32), 'beta2': jnp.zeros((D,), dtype=jnp.float32)}
        return inp
    _L1_cond_all = _L1_cond_setup()
    _L1_cond_in = {k: v for k, v in _L1_cond_all.items() if k in ('W_ada', 'b_ada', 'Wq', 'bq', 'Wk', 'bk', 'Wv', 'bv', 'Wo', 'bo', 'W1', 'b1', 'W2', 'b2', 'g2', 'beta2')}
    del _L1_cond_all

    def _L2_cond_setup():
        import jax, jax.numpy as jnp
        import numpy as np
        B, S, D = (32, 512, 512)
        A = 128
        E = 16
        LN_EPS = 1e-05
        key = jax.random.key(seed)
        ks = jax.random.split(key, 10)
        s = lambda fan_in: 1.0 / np.sqrt(fan_in)
        return {'hidden_states': jax.random.normal(ks[0], (B, S, D), dtype=jnp.float32), 'domain_id': jax.random.randint(ks[1], (B,), 0, E, dtype=jnp.int64), 'down_W': jax.random.uniform(ks[2], (A, D), jnp.float32, -s(D), s(D)), 'down_b': jax.random.uniform(ks[3], (A,), jnp.float32, -s(D), s(D)), 'up_W': jax.random.uniform(ks[4], (D, A), jnp.float32, -s(A), s(A)), 'up_b': jax.random.uniform(ks[5], (D,), jnp.float32, -s(A), s(A)), 'expert_W': jax.random.uniform(ks[6], (E, A, A), jnp.float32, -s(A), s(A)), 'expert_b': jax.random.uniform(ks[7], (E, A), jnp.float32, -s(A), s(A)), 'domain_emb': jax.random.normal(ks[8], (E, A), dtype=jnp.float32), 'ln_gamma': jnp.ones((D,), jnp.float32), 'ln_beta': jnp.zeros((D,), jnp.float32)}
    _L2_cond_all = _L2_cond_setup()
    _L2_cond_in = {k: v for k, v in _L2_cond_all.items() if k in ('down_W', 'down_b', 'up_W', 'up_b', 'expert_W', 'expert_b', 'domain_emb', 'ln_gamma', 'ln_beta')}
    del _L2_cond_all

    def _L3_cond_setup():
        import jax, jax.numpy as jnp
        import numpy as np
        B, NX, NY = (16, 512, 512)

        def _grad(f, axis):
            fm = jnp.moveaxis(f, axis, -1)
            g = (jnp.roll(fm, -1, -1) - jnp.roll(fm, 1, -1)) * 0.5
            g0 = (-3.0 * fm[..., 0] + 4.0 * fm[..., 1] - fm[..., 2]) * 0.5
            gN = (3.0 * fm[..., -1] - 4.0 * fm[..., -2] + fm[..., -3]) * 0.5
            g = g.at[..., 0].set(g0).at[..., -1].set(gN)
            return jnp.moveaxis(g, -1, axis)

        def _grad2(f, axis):
            fm = jnp.moveaxis(f, axis, -1)
            g = jnp.roll(fm, -1, -1) - 2.0 * fm + jnp.roll(fm, 1, -1)
            g0 = 2.0 * fm[..., 0] - 5.0 * fm[..., 1] + 4.0 * fm[..., 2] - fm[..., 3]
            gN = 2.0 * fm[..., -1] - 5.0 * fm[..., -2] + 4.0 * fm[..., -3] - fm[..., -4]
            g = g.at[..., 0].set(g0).at[..., -1].set(gN)
            return jnp.moveaxis(g, -1, axis)
        key = jax.random.key(seed)
        k1, k2, k3, k4 = jax.random.split(key, 4)
        f = jax.random.uniform(k1, (B, NX, NY), dtype=jnp.float32)
        A_grid = jax.random.normal(k2, (2, NX, NY), dtype=jnp.float32)
        B_grid = jax.random.uniform(k3, (3, NX, NY), dtype=jnp.float32)
        dt = jax.random.uniform(k4, (B,), dtype=jnp.float32)
        return {'f': f, 'A_grid': A_grid, 'B_grid': B_grid, 'dt': dt}
    _L3_cond_all = _L3_cond_setup()
    _L3_cond_in = {k: v for k, v in _L3_cond_all.items() if k in ('A_grid', 'B_grid')}
    del _L3_cond_all
    return {'x': x, 'condB_theta': condB_theta, 'condB_phi': condB_phi, 'itok_B_34_63': itok_B_34_63, 'fside_Bx16xSxS_0': fside_Bx16xSxS_0, 'itok_B_0_15': itok_B_0_15, 'condB_dt': condB_dt, 'mask_Bx1xSxS_bk0': mask_Bx1xSxS_bk0, 'L1_cond_W_ada': _L1_cond_in['W_ada'], 'L1_cond_b_ada': _L1_cond_in['b_ada'], 'L1_cond_Wq': _L1_cond_in['Wq'], 'L1_cond_bq': _L1_cond_in['bq'], 'L1_cond_Wk': _L1_cond_in['Wk'], 'L1_cond_bk': _L1_cond_in['bk'], 'L1_cond_Wv': _L1_cond_in['Wv'], 'L1_cond_bv': _L1_cond_in['bv'], 'L1_cond_Wo': _L1_cond_in['Wo'], 'L1_cond_bo': _L1_cond_in['bo'], 'L1_cond_W1': _L1_cond_in['W1'], 'L1_cond_b1': _L1_cond_in['b1'], 'L1_cond_W2': _L1_cond_in['W2'], 'L1_cond_b2': _L1_cond_in['b2'], 'L1_cond_g2': _L1_cond_in['g2'], 'L1_cond_beta2': _L1_cond_in['beta2'], 'L2_cond_down_W': _L2_cond_in['down_W'], 'L2_cond_down_b': _L2_cond_in['down_b'], 'L2_cond_up_W': _L2_cond_in['up_W'], 'L2_cond_up_b': _L2_cond_in['up_b'], 'L2_cond_expert_W': _L2_cond_in['expert_W'], 'L2_cond_expert_b': _L2_cond_in['expert_b'], 'L2_cond_domain_emb': _L2_cond_in['domain_emb'], 'L2_cond_ln_gamma': _L2_cond_in['ln_gamma'], 'L2_cond_ln_beta': _L2_cond_in['ln_beta'], 'L3_cond_A_grid': _L3_cond_in['A_grid'], 'L3_cond_B_grid': _L3_cond_in['B_grid']}

def reference(x, condB_theta, condB_phi, itok_B_34_63, fside_Bx16xSxS_0, itok_B_0_15, condB_dt, mask_Bx1xSxS_bk0, L1_cond_W_ada, L1_cond_b_ada, L1_cond_Wq, L1_cond_bq, L1_cond_Wk, L1_cond_bk, L1_cond_Wv, L1_cond_bv, L1_cond_Wo, L1_cond_bo, L1_cond_W1, L1_cond_b1, L1_cond_W2, L1_cond_b2, L1_cond_g2, L1_cond_beta2, L2_cond_down_W, L2_cond_down_b, L2_cond_up_W, L2_cond_up_b, L2_cond_expert_W, L2_cond_expert_b, L2_cond_domain_emb, L2_cond_ln_gamma, L2_cond_ln_beta, L3_cond_A_grid, L3_cond_B_grid):
    import jax
    import jax.numpy as jnp

    def _L0_cond_ref(embeddings, theta, phi):
        import jax, jax.numpy as jnp
        import numpy as np
        B, N, D = embeddings.shape
        e = embeddings.reshape(B, N, D // 4, 4)
        ct = jnp.cos(theta)[:, None, None]
        st = jnp.sin(theta)[:, None, None]
        cp = jnp.cos(phi)[:, None, None]
        sp = jnp.sin(phi)[:, None, None]
        x0, x1, x2, x3 = (e[..., 0], e[..., 1], e[..., 2], e[..., 3])
        out = jnp.stack([x0 * ct + x1 * st, -x0 * st + x1 * ct, x2 * cp + x3 * sp, -x2 * sp + x3 * cp], axis=-1)
        return out.reshape(B, N, D)

    def _L1_cond_ref(src, src_mask, timestep, attention_bias, W_ada, b_ada, Wq, bq, Wk, bk, Wv, bv, Wo, bo, W1, b1, W2, b2, g2, beta2):
        import jax, jax.numpy as jnp
        import numpy as np
        import math
        D_MODEL = 512
        N_HEAD = 16
        HEAD_DIM = D_MODEL // N_HEAD
        D_FF = 2048
        NUM_STEPS = 100.0
        RESCALE = 4000.0
        EPS = 1e-05

        def _sin_emb(t):
            half = D_MODEL // 2
            x = t.astype(jnp.float32) / NUM_STEPS * RESCALE
            freqs = jnp.exp(jnp.arange(half, dtype=jnp.float32) * (-math.log(10000.0) / (half - 1)))
            e = x[:, None] * freqs[None, :]
            return jnp.concatenate([jnp.sin(e), jnp.cos(e)], axis=-1)

        def _ln(x):
            m = jnp.mean(x, axis=-1, keepdims=True)
            v = jnp.var(x, axis=-1, keepdims=True)
            return (x - m) / jnp.sqrt(v + EPS)

        def _gelu2(x):
            return x * jax.nn.sigmoid(1.702 * x)
        B, S, D = src.shape
        emb = jax.nn.silu(_sin_emb(timestep)) @ W_ada + b_ada
        scale, shift = jnp.split(emb[:, None, :], 2, axis=-1)
        x = _ln(src) * (1.0 + scale) + shift
        q = (x @ Wq + bq).reshape(B, S, N_HEAD, HEAD_DIM).transpose(0, 2, 1, 3)
        k = (x @ Wk + bk).reshape(B, S, N_HEAD, HEAD_DIM).transpose(0, 2, 1, 3)
        v = (x @ Wv + bv).reshape(B, S, N_HEAD, HEAD_DIM).transpose(0, 2, 1, 3)
        scores = jnp.einsum('bhqd,bhkd->bhqk', q / math.sqrt(HEAD_DIM), k)
        scores = scores + attention_bias
        scores = jnp.where(src_mask, -jnp.inf, scores.astype(jnp.float32))
        probs = jax.nn.softmax(scores, axis=-1).astype(v.dtype)
        ctx = jnp.einsum('bhqk,bhkd->bhqd', probs, v)
        ctx = ctx.transpose(0, 2, 1, 3).reshape(B, S, D)
        x = x + (ctx @ Wo + bo)
        h = _ln(x) * g2 + beta2
        ff = _gelu2(h @ W1 + b1) @ W2 + b2
        return x + ff

    def _L2_cond_ref(hidden_states, domain_id, down_W, down_b, up_W, up_b, expert_W, expert_b, domain_emb, ln_gamma, ln_beta):
        import jax, jax.numpy as jnp
        import numpy as np
        B, S, D = (32, 512, 512)
        A = 128
        E = 16
        LN_EPS = 1e-05
        residual = hidden_states
        hidden = jnp.einsum('bsd,ad->bsa', hidden_states, down_W) + down_b
        hidden = jax.nn.gelu(hidden, approximate=False)
        valid = (domain_id >= 0) & (domain_id < E)
        idx = jnp.clip(domain_id, 0, E - 1)
        Wsel = expert_W[idx]
        bsel = expert_b[idx]
        expert_out = jnp.einsum('bsa,boa->bso', hidden, Wsel) + bsel[:, None, :]
        domain_output = jnp.where(valid[:, None, None], expert_out, hidden)
        hidden = domain_output + domain_emb[idx][:, None, :]
        hidden = jnp.einsum('bsa,da->bsd', hidden, up_W) + up_b
        x = hidden + residual
        mu = jnp.mean(x, axis=-1, keepdims=True)
        var = jnp.mean(jnp.square(x - mu), axis=-1, keepdims=True)
        return (x - mu) * jax.lax.rsqrt(var + LN_EPS) * ln_gamma + ln_beta

    def _L3_cond_ref(f, A_grid, B_grid, dt):
        import jax, jax.numpy as jnp
        import numpy as np
        B, NX, NY = (16, 512, 512)

        def _grad(f, axis):
            fm = jnp.moveaxis(f, axis, -1)
            g = (jnp.roll(fm, -1, -1) - jnp.roll(fm, 1, -1)) * 0.5
            g0 = (-3.0 * fm[..., 0] + 4.0 * fm[..., 1] - fm[..., 2]) * 0.5
            gN = (3.0 * fm[..., -1] - 4.0 * fm[..., -2] + fm[..., -3]) * 0.5
            g = g.at[..., 0].set(g0).at[..., -1].set(gN)
            return jnp.moveaxis(g, -1, axis)

        def _grad2(f, axis):
            fm = jnp.moveaxis(f, axis, -1)
            g = jnp.roll(fm, -1, -1) - 2.0 * fm + jnp.roll(fm, 1, -1)
            g0 = 2.0 * fm[..., 0] - 5.0 * fm[..., 1] + 4.0 * fm[..., 2] - fm[..., 3]
            gN = 2.0 * fm[..., -1] - 5.0 * fm[..., -2] + 4.0 * fm[..., -3] - fm[..., -4]
            g = g.at[..., 0].set(g0).at[..., -1].set(gN)
            return jnp.moveaxis(g, -1, axis)
        Af = A_grid[None] * f[:, None]
        Bf = B_grid[None] * f[:, None]
        gradv_Af = _grad(Af[:, 0], 1) + _grad(Af[:, 1], 2)
        gradvv_Bf = _grad2(Bf[:, 0], 1) + _grad2(Bf[:, 1], 2) + _grad(_grad(Bf[:, 2], 2), 1) + _grad(_grad(Bf[:, 2], 1), 2)
        df = -gradv_Af + gradvv_Bf * 0.5
        f_new = f + df * dt[:, None, None]
        return jnp.maximum(f_new, 0.0)
    x = _L0_cond_ref(x, condB_theta, condB_phi)
    x = _L1_cond_ref(x, mask_Bx1xSxS_bk0, itok_B_34_63, fside_Bx16xSxS_0, L1_cond_W_ada, L1_cond_b_ada, L1_cond_Wq, L1_cond_bq, L1_cond_Wk, L1_cond_bk, L1_cond_Wv, L1_cond_bv, L1_cond_Wo, L1_cond_bo, L1_cond_W1, L1_cond_b1, L1_cond_W2, L1_cond_b2, L1_cond_g2, L1_cond_beta2)
    x = _L2_cond_ref(x, itok_B_0_15, L2_cond_down_W, L2_cond_down_b, L2_cond_up_W, L2_cond_up_b, L2_cond_expert_W, L2_cond_expert_b, L2_cond_domain_emb, L2_cond_ln_gamma, L2_cond_ln_beta)
    x = _L3_cond_ref(x, L3_cond_A_grid, L3_cond_B_grid, condB_dt)
    return x

_drawn_inputs = setup_inputs


def setup_inputs(seed=0):
    import zlib

    import numpy as np

    out = dict(_drawn_inputs(seed))
    spreads = {'L1_cond_b_ada': (0.0, 0.1),
     'L1_cond_bq': (0.0, 0.8),
     'L1_cond_bk': (0.0, 0.8),
     'L1_cond_bv': (0.0, 0.1),
     'L1_cond_bo': (0.0, 0.1),
     'L1_cond_b1': (0.0, 0.1),
     'L1_cond_b2': (0.0, 0.1),
     'L1_cond_g2': (1.0, 0.2),
     'L1_cond_beta2': (0.0, 0.377),
     'L2_cond_ln_gamma': (1.0, 0.2),
     'L2_cond_ln_beta': (0.0, 0.1)}
    factors = {'fside_Bx16xSxS_0': 5.396, 'L1_cond_Wq': 8.0, 'L1_cond_Wk': 8.0, 'L2_cond_down_b': 8.0}
    for name, (base, spread) in spreads.items():
        noise = np.random.default_rng([zlib.crc32(name.encode()), seed]).standard_normal(out[name].shape)
        drawn = base * np.exp(spread * noise) if base else spread * noise
        out[name] = jnp.asarray(drawn.astype(out[name].dtype))
    for name, factor in factors.items():
        out[name] = (out[name] * factor).astype(out[name].dtype)
    return out
```

```python
import math
from contextlib import ExitStack

import concourse.bass as bass
import concourse.mybir as mybir
from concourse.alu_op_type import AluOpType as ALU

ACT = mybir.ActivationFunctionType
F32 = mybir.dt.float32
I32 = mybir.dt.int32
U8 = mybir.dt.uint8

P = 128
S = 512
D = 512
T = S // P
DT = D // P
HEADS = 16
DH = D // HEADS
GH = P // DH
GROUPS = HEADS // GH
STEPS = GROUPS * T
UNITS = STEPS * GH
FF = 2048
FT = FF // P
ADP = 128
EXPERTS = 16
MASKED = -1.0e30
EPS = 1e-5
HALF = D // 2
COND = 2 * D + 4

START = 1

TWO_PI_A = 6.28125
TWO_PI_B = 0.00193500518798828125
TWO_PI_C = 2 * math.pi - TWO_PI_A - TWO_PI_B
ROUND = 1.5 * 2.0 ** 23
PI_IN = 3.1415925


def apart(engine, passed):
    engine.sem_inc(passed, 1)


def identity(nc, pool, ident, zeroed):
    nc.gpsimd.memset(ident[:, :], 0.0).then_inc(zeroed, 1)
    pool.wait_ge(zeroed, 1)
    return nc.gpsimd.affine_select(out=ident[:, :], in_=ident[:, :], compare_op=ALU.not_equal, fill=1.0,
                                   base=0, pattern=[[-1, P]], channel_multiplier=1)


def setup(nc, a, cond_dram, bias_dram):
    B = a["x"].shape[0]
    with ExitStack() as ctx:
        def sb(name, shape, dt=F32):
            return ctx.enter_context(nc.sbuf_tensor("su_" + name, shape, dt))

        def sem(name):
            return ctx.enter_context(nc.semaphore("su_" + name))

        ident = sb("ident", [P, P])
        w_ada = sb("w_ada", [P, DT, 2 * D])
        wo = sb("wo", [P, DT, D])
        bv = sb("bv", [P, DT])
        bo = sb("bo", [P, D])
        b_ada = sb("b_ada", [B, 2 * D])
        freqs = sb("freqs", [B, HALF])
        step_i = sb("step_i", [B, 1], I32)
        step_x = sb("step_x", [B, 2])
        angle = sb("angle", [B, 2, HALF + 2])
        turns = sb("turns", [B, 2, HALF + 2])
        waves = sb("waves", [B, 2, HALF + 2])
        silu = sb("silu", [B, D])
        silu_t = sb("silu_t", [P, DT, B])
        cond = sb("cond", [B, COND])
        bias = sb("bias", [P, D])
        ps_t = ctx.enter_context(nc.psum_tensor("su_ps_t", [P, 512], F32))
        ps_c = ctx.enter_context(nc.psum_tensor("su_ps_c", [P, 2, 512], F32))
        ps_b = ctx.enter_context(nc.psum_tensor("su_ps_b", [P, 512], F32))
        small_in, wada_in, wo_in = sem("small_in"), sem("wada_in"), sem("wo_in")
        zeroed, ident_made, chain, waved = sem("zeroed"), sem("ident_made"), sem("chain"), sem("waved")
        turned, turned_out, cond_mm, bias_mm = sem("turned"), sem("turned_out"), sem("cond_mm"), sem("bias_mm")
        rows_done, stored = sem("rows_done"), sem("stored")
        SMALL = 7

        with nc.Block() as block:
            @block.sync
            def _(sp):
                sp.dma_start(step_i[:, :], a["itok_B_34_63"].rearrange("(b o) -> b o", o=1)).then_inc(small_in, 16)
                sp.dma_start(freqs[:, :], a["freqs"].partition_broadcast(B)).then_inc(small_in, 16)
                for c in range(2):
                    sp.dma_start(angle[:, c, HALF:HALF + 1], a["condB_theta"].rearrange("(b o) -> b o", o=1)).then_inc(small_in, 16)
                    sp.dma_start(angle[:, c, HALF + 1:HALF + 2], a["condB_phi"].rearrange("(b o) -> b o", o=1)).then_inc(small_in, 16)
                sp.dma_start(b_ada[:, :], a["L1_cond_b_ada"].partition_broadcast(B)).then_inc(small_in, 16)
                sp.dma_start(w_ada[:, :, :], a["L1_cond_W_ada"].rearrange("(t p) n -> p t n", p=P)).then_inc(wada_in, 16)
                sp.dma_start(wo[:, :, :], a["L1_cond_Wo"].rearrange("(t p) n -> p t n", p=P)).then_inc(wo_in, 16)
                sp.dma_start(bv[:, :], a["L1_cond_bv"].rearrange("(t p) -> p t", p=P), allow_slow_non_contiguous=True).then_inc(wo_in, 16)
                sp.dma_start(bo[:, :], a["L1_cond_bo"].partition_broadcast(P)).then_inc(wo_in, 16)
                sp.wait_ge(rows_done, 2)
                sp.dma_start(cond_dram, cond[:, :]).then_inc(stored, 16)
                sp.dma_start(bias_dram, bias[:, :]).then_inc(stored, 16)
                sp.wait_ge(stored, 32)

            @block.gpsimd
            def _(pool):
                identity(nc, pool, ident, zeroed).then_inc(ident_made, 1)

            @block.vector
            def _(dve):
                done = [0]

                def then(ins):
                    ins.then_inc(chain, 1)
                    done[0] += 1
                    dve.wait_ge(chain, done[0])

                v = nc.vector
                dve.wait_ge(small_in, 16 * SMALL)
                then(v.tensor_copy(step_x[:, 0:1], step_i[:, :]))
                then(v.tensor_scalar(step_x[:, 1:2], step_x[:, 0:1], 40.0, None, ALU.mult))
                for c in range(2):
                    then(v.tensor_scalar(angle[:, c, 0:HALF], freqs[:, :], step_x[:, 1:2], None, ALU.mult))
                for c in range(2):
                    then(v.tensor_scalar(turns[:, c, :], angle[:, c, :], 1 / (2 * math.pi), 0.25 * c, ALU.mult, ALU.add))
                then(v.tensor_scalar(turns[:, :, :], turns[:, :, :], ROUND, None, ALU.add))
                then(v.tensor_scalar(turns[:, :, :], turns[:, :, :], ROUND, None, ALU.subtract))
                for part in (TWO_PI_A, TWO_PI_B, TWO_PI_C):
                    then(v.scalar_tensor_tensor(angle[:, :, :], turns[:, :, :], -part, angle[:, :, :], ALU.mult, ALU.add))
                then(v.tensor_scalar(angle[:, 1, :], angle[:, 1, :], math.pi / 2, None, ALU.add))
                then(v.tensor_scalar(angle[:, :, :], angle[:, :, :], PI_IN, -PI_IN, ALU.min, ALU.max))
                dve.wait_ge(turned, 1)
                v.tensor_copy(silu_t[:, :, :].rearrange("p t b -> p (t b)"), ps_t[:, 0:DT * B]).then_inc(turned_out, 1)
                dve.wait_ge(cond_mm, 1)
                v.tensor_tensor(cond[:, 0:2 * D].rearrange("b (c n) -> b c n", c=2), ps_c[0:B, :, :],
                                b_ada[:, :].rearrange("b (c n) -> b c n", c=2), ALU.add).then_inc(chain, 1)
                dve.wait_ge(chain, done[0] + 1)
                v.tensor_scalar(cond[:, 0:D], cond[:, 0:D], 1.0, None, ALU.add).then_inc(chain, 1)
                v.tensor_copy(cond[:, 2 * D:2 * D + 4].rearrange("b (c n) -> b c n", c=2),
                              waves[:, :, HALF:HALF + 2]).then_inc(rows_done, 1)
                dve.wait_ge(bias_mm, 1)
                v.tensor_tensor(bias[:, :], ps_b[:, :], bo[:, :], ALU.add).then_inc(rows_done, 1)
                done_chain = done[0]

            @block.scalar
            def _(act):
                act.wait_ge(chain, 13)
                nc.scalar.activation(waves[:, :, :], angle[:, :, :], ACT.Sin).then_inc(waved, 1)
                act.wait_ge(waved, 1)
                nc.scalar.activation(silu[:, :].rearrange("b (c n) -> b c n", c=2), waves[:, :, 0:HALF],
                                     ACT.Silu).then_inc(waved, 1)

            @block.tensor
            def _(pe):
                pe.wait_ge(ident_made, 1)
                pe.wait_ge(waved, 2)
                for t in range(DT):
                    last = nc.tensor.transpose(ps_t[:, t * B:(t + 1) * B], silu[:, t * P:(t + 1) * P], ident[0:B, 0:B])
                last.then_inc(turned, 1)
                pe.wait_ge(turned_out, 1)
                pe.wait_ge(wada_in, 16)
                for c in range(2):
                    for t in range(DT):
                        last = nc.tensor.matmul(ps_c[0:B, c, :], silu_t[:, t, :], w_ada[:, t, c * D:(c + 1) * D],
                                                start=(t == 0), stop=(t == DT - 1))
                last.then_inc(cond_mm, 1)
                pe.wait_ge(wo_in, 48)
                for t in range(DT):
                    last = nc.tensor.matmul(ps_b[:, :], bv[:, t:t + 1].to_broadcast([P, P]), wo[:, t, :],
                                            start=(t == 0), stop=(t == DT - 1))
                last.then_inc(bias_mm, 1)


def attention(nc, a, cond_dram, bias_dram, x1_dram):
    B = a["x"].shape[0]
    with ExitStack() as ctx:
        def sb(name, shape, dt=F32):
            return ctx.enter_context(nc.sbuf_tensor("at_" + name, shape, dt))

        def sem(name):
            return ctx.enter_context(nc.semaphore("at_" + name))

        def bank(name):
            return ctx.enter_context(nc.psum_tensor("at_" + name, [P, 512], F32))

        ident = sb("ident", [P, P])
        wq, wk, wv, wo = (sb(n, [P, DT, D]) for n in ("wq", "wk", "wv", "wo"))
        bq_raw, bq, bk = sb("bq_raw", [P, GROUPS]), sb("bq", [P, GROUPS]), sb("bk", [P, GROUPS])
        bo = sb("bo", [P, D])
        power, eps = sb("power", [P, T]), sb("eps", [P, T])
        x_in = sb("x_in", [P, T, D])
        cond = sb("cond", [P, COND])
        rot_a, rot_b = sb("rot_a", [P, D]), sb("rot_b", [P, D])
        stats = sb("stats", [P, T, 6])
        moments = sb("moments", [P, T, 2])
        rstd = sb("rstd", [P, T])
        xn = sb("xn", [P, T, D])
        residual = sb("residual", [P, T, D])
        mask_in = sb("mask_in", [P, T, S], U8)
        masked_add = sb("masked_add", [P, T, S])
        xt = sb("xt", [P, DT, S])
        v_sb = sb("v_sb", [P, T, D])
        qt = [sb(f"qt{i}", [P, S]) for i in range(2)]
        kt = [sb(f"kt{i}", [P, S]) for i in range(2)]
        RING = 4
        passed = ctx.enter_context(nc.semaphore("at_passed"))
        probs = [sb(f"probs{i}", [P, GH, S]) for i in range(RING)]
        probs_t = [sb(f"probs_t{i}", [P, GH, T, P]) for i in range(2)]
        neg_max = [sb(f"neg_max{i}", [P, GH]) for i in range(2)]
        sums = [sb(f"sums{i}", [P, GH]) for i in range(2)]
        spoilt = [sb(f"spoilt{i}", [P, GH]) for i in range(2)]
        recip = [sb(f"recip{i}", [P, GH]) for i in range(2)]
        recip_b = [sb(f"recip_b{i}", [P, P]) for i in range(2)]
        ctx_t = sb("ctx_t", [P, GROUPS, S])

        ps_s = [bank(f"ps_s{i}") for i in range(2)]
        ps_p = [bank(f"ps_p{i}") for i in range(2)]
        ps_x = [bank(f"ps_x{i}") for i in range(2)]
        ps_m = [bank(f"ps_m{i}") for i in range(2)]

        weights_in, zeroed, ident_made, consts = sem("weights_in"), sem("zeroed"), sem("ident_made"), sem("consts")
        x_landed, cond_landed, mask_landed = sem("x_landed"), sem("cond_landed"), sem("mask_landed")
        bias_landed = [sem(f"bias_landed{i}") for i in range(RING)]
        mask_made, bias_masked = sem("mask_made"), sem("bias_masked")
        norm_chain, rstd_made, xn_ready, residual_made = sem("norm_chain"), sem("rstd_made"), sem("xn_ready"), sem("residual_made")
        mod_chain = sem("mod_chain")
        job_filled = [sem(f"job_filled{i}") for i in range(2)]
        job_taken = [sem(f"job_taken{i}") for i in range(2)]
        scores_ready, scores_biased, probs_ready = sem("scores_ready"), sem("scores_biased"), sem("probs_ready")
        probs_turned = sem("probs_turned")
        turned_taken = [sem(f"turned_taken{i}") for i in range(2)]
        recip_made, recip_ready, recip_spread, recip_copied = sem("recip_made"), sem("recip_ready"), sem("recip_spread"), sem("recip_copied")
        spoil_chain = sem("spoil_chain")
        ctx_ready, ctx_taken, x1_made, x1_stored = sem("ctx_ready"), sem("ctx_taken"), sem("x1_made"), sem("x1_stored")

        JOBS = 4 + T + 2 * GROUPS + T
        NJ = JOBS // 2
        JOB_X, JOB_V, JOB_QK, JOB_O = 0, DT, DT + T, DT + T + 2 * GROUPS
        NORM = 8 + 3 * T

        bias_dram_tiles = a["fside_Bx16xSxS_0"].rearrange("b (g h) (p t) k -> b g t p h k", h=GH, t=T)

        def q_slot(g):
            return (g - 1) * T * GH + 7

        with nc.Block() as block:
            @block.sync
            def _(sp):
                for counted in [*job_taken, *turned_taken, x1_stored, mod_chain, norm_chain]:
                    sp.sem_inc(counted, START)
                for w, n in ((wq, "Wq"), (wk, "Wk"), (wv, "Wv"), (wo, "Wo")):
                    sp.dma_start(w[:, :, :], a["L1_cond_" + n].rearrange("(t p) n -> p t n", p=P)).then_inc(weights_in, 16)
                sp.dma_start(bq_raw[:, :], a["L1_cond_bq"].rearrange("(t p) -> p t", p=P), allow_slow_non_contiguous=True).then_inc(weights_in, 16)
                sp.dma_start(bk[:, :], a["L1_cond_bk"].rearrange("(t p) -> p t", p=P), allow_slow_non_contiguous=True).then_inc(weights_in, 16)
                sp.dma_start(bo[:, :], bias_dram).then_inc(weights_in, 16)

                def next_inputs(n):
                    sp.dma_start(x_in[:, :, :], a["x"][n].rearrange("(p t) d -> p t d", t=T)).then_inc(x_landed, 16)
                    sp.dma_start(cond[:, :], cond_dram[n].partition_broadcast(P)).then_inc(cond_landed, 16)
                    sp.dma_start(mask_in[:, :, :], a["mask_Bx1xSxS_bk0"][n, 0].rearrange("(p t) k -> p t k", t=T)).then_inc(mask_landed, 16)

                next_inputs(0)
                with sp.Fori(0, B) as b:
                    following = sp.snap((b + 1) % B)
                    for s in range(STEPS):
                        if s == 4:
                            sp.wait_ge(norm_chain, START + NORM * b + NORM)
                            apart(sp, passed)
                            sp.wait_ge(xn_ready, b + 1)
                            sp.wait_ge(mask_made, b + 1)
                            apart(sp, passed)
                            next_inputs(following)
                        sp.wait_ge(probs_turned, UNITS * b + GH * (s + 1))
                        apart(sp, passed)
                        sp.dma_start(probs[s % RING][:, :, :], bias_dram_tiles[b, s // T, s % T]).then_inc(bias_landed[s % RING], 16)
                sp.wait_ge(x1_stored, START + 16 * B)

            @block.gpsimd
            def _(pool):
                g_ = nc.gpsimd
                identity(nc, pool, ident, zeroed).then_inc(ident_made, 1)
                g_.memset(power[:, :], -0.5).then_inc(consts, 1)
                g_.memset(eps[:, :], EPS).then_inc(consts, 1)

                def inverse_deviation(n):
                    pool.wait_ge(norm_chain, START + NORM * n + 8 + 2 * T)
                    pool.wait_ge(mod_chain, START + 4 * n)
                    g_.tensor_tensor(rstd[:, :], moments[:, :, 1], eps[:, :], ALU.add).then_inc(mod_chain, 1)
                    pool.wait_ge(mod_chain, START + 4 * n + 1)
                    g_.tensor_tensor(rstd[:, :], rstd[:, :], power[:, :], ALU.pow).then_inc(rstd_made, 1)

                def modulate(n):
                    pool.wait_ge(norm_chain, START + NORM * n + NORM)
                    pool.wait_ge(rstd_made, n + 1)
                    scale = cond[:, 0:D].unsqueeze(1).to_broadcast([P, T, D])
                    shift = cond[:, D:2 * D].unsqueeze(1).to_broadcast([P, T, D])
                    g_.tensor_tensor(xn[:, :, :], xn[:, :, :], scale, ALU.mult).then_inc(mod_chain, 1)
                    pool.wait_ge(mod_chain, START + 4 * n + 2)
                    g_.tensor_tensor(xn[:, :, :], xn[:, :, :], shift, ALU.add).then_inc(xn_ready, 1)
                    pool.wait_ge(xn_ready, n + 1)
                    g_.nop().then_inc(mod_chain, 2)

                def mask_step(b, s):
                    if s == 0:
                        pool.wait_ge(mask_made, b + 1)
                    pool.wait_ge(bias_landed[s % RING], 16 * (STEPS // RING) * b + 16 * (s // RING + 1))
                    g_.tensor_tensor(probs[s % RING][:, :, :], probs[s % RING][:, :, :],
                                     masked_add[:, s % T, :].unsqueeze(1).to_broadcast([P, GH, S]),
                                     ALU.add).then_inc(bias_masked, 1)

                def residual_of(b):
                    pool.wait_ge(x1_stored, START + 16 * b)
                    g_.tensor_tensor(residual[:, :, :], xn[:, :, :], bo[:, :].unsqueeze(1).to_broadcast([P, T, D]),
                                     ALU.add).then_inc(residual_made, 1)

                pool.wait_ge(consts, 3)
                inverse_deviation(0)
                modulate(0)
                pool.wait_ge(weights_in, 16 * 7)
                with pool.Fori(0, B) as b:
                    for s in range(STEPS):
                        mask_step(b, s)
                        if s == 1:
                            residual_of(b)
                        if s == 11:
                            inverse_deviation(b + 1)
                        if s == 13:
                            modulate(b + 1)

            def norm_steps(dve, v, n):
                k = [0]

                def link(ins):
                    ins.then_inc(norm_chain, 1)
                    k[0] += 1

                def ready():
                    dve.wait_ge(norm_chain, START + NORM * n + k[0])

                x4 = x_in[:, :, :].rearrange("p t (f c) -> p (t f) c", c=4)
                y4 = xn[:, :, :].rearrange("p t (f c) -> p (t f) c", c=4)
                sin, cos = cond[:, 2 * D:2 * D + 2], cond[:, 2 * D + 2:2 * D + 4]
                for c in range(2):
                    first, second = x4[:, :, 2 * c], x4[:, :, 2 * c + 1]
                    ready()
                    if c == 0:
                        dve.wait_ge(x_landed, 16 * n + 16)
                        dve.wait_ge(cond_landed, 16 * n + 16)
                    link(v.tensor_scalar(rot_a[:, :], second, sin[:, c:c + 1], None, ALU.mult))
                    yield
                    link(v.tensor_scalar(rot_b[:, :], first, sin[:, c:c + 1], None, ALU.mult))
                    yield
                    ready()
                    link(v.scalar_tensor_tensor(y4[:, :, 2 * c], first, cos[:, c:c + 1], rot_a[:, :], ALU.mult, ALU.add))
                    yield
                    link(v.scalar_tensor_tensor(y4[:, :, 2 * c + 1], second, cos[:, c:c + 1], rot_b[:, :], ALU.mult, ALU.subtract))
                    yield
                ready()
                for t in range(T):
                    link(v.bn_stats(stats[:, t, :], xn[:, t, :]))
                    yield
                ready()
                apart(dve, passed)
                for t in range(T):
                    link(v.bn_aggr(moments[:, t, :], stats[:, t, :]))
                yield
                yield
                yield
                yield
                dve.wait_ge(rstd_made, n + 1)
                ready()
                for t in range(T):
                    link(v.tensor_scalar(xn[:, t, :], xn[:, t, :], moments[:, t, 0:1], rstd[:, t:t + 1],
                                         ALU.subtract, ALU.mult))
                    yield

            @block.vector
            def _(dve):
                v = nc.vector
                dve.wait_ge(weights_in, 16 * 7)
                v.tensor_scalar(bq[:, :], bq_raw[:, :], DH ** -0.5, None, ALU.mult).then_inc(consts, 1)
                dve.sem_inc(ctx_taken, 2)
                for _ in norm_steps(dve, v, 0):
                    pass

                def take_job(b, job, out, scale=None, bias=None, add=None):
                    i = job % 2
                    dve.wait_ge(job_filled[i], NJ * b + job // 2 + 1)
                    if add is not None:
                        return v.tensor_tensor(out, ps_m[i][:, :], add, ALU.add)
                    if bias is not None:
                        return v.tensor_scalar(out, ps_m[i][:, :], bias, None, ALU.add).then_inc(job_taken[i], 1)
                    return v.tensor_copy(out, ps_m[i][:, :]).then_inc(job_taken[i], 1)

                def bias_and_max(b, u):
                    s, h = u // GH, u % GH
                    dve.wait_ge(scores_ready, UNITS * b + u + 1)
                    if h == 0:
                        dve.wait_ge(bias_masked, STEPS * b + s + 1)
                    apart(dve, passed)
                    tile = probs[s % RING][:, h, :].rearrange("p (k t) -> p t k", t=T)
                    v.tensor_tensor_reduce(tile, ps_s[u % 2][:, :].rearrange("p (t k) -> p t k", t=T), tile,
                                           -1.0, 3.0e38, ALU.add, ALU.min,
                                           neg_max[s % 2][:, h:h + 1]).then_inc(scores_biased, 1)

                def take_turned(b, u):
                    s, h = u // GH, u % GH
                    dve.wait_ge(probs_turned, UNITS * b + u + 1 + RING * GH)
                    if h == 1:
                        dve.wait_ge(ctx_ready, STEPS * b + s + 1)
                    v.tensor_copy(probs_t[s % 2][:, h, :, :].rearrange("p t k -> p (t k)"),
                                  ps_p[u % 2][:, :]).then_inc(turned_taken[u % 2], 1)

                def reciprocal(b, s):
                    dve.wait_ge(probs_ready, UNITS * b + GH * (s + 1))
                    i = s % 2
                    n = 3 * (STEPS * b + s)
                    v.tensor_scalar(spoilt[i][:, :], neg_max[i][:, :], 1.0e10, None, ALU.mult).then_inc(recip_made, 1)
                    v.reciprocal(recip[i][:, :], sums[i][:, :]).then_inc(recip_made, 1)
                    dve.wait_ge(recip_made, n + 2)
                    v.scalar_tensor_tensor(spoilt[i][:, :], neg_max[i][:, :], 1.0e10, spoilt[i][:, :],
                                           ALU.mult, ALU.subtract).then_inc(recip_made, 1)
                    dve.wait_ge(recip_made, n + 3)
                    v.tensor_tensor(recip[i][:, :], recip[i][:, :], spoilt[i][:, :], ALU.add).then_inc(recip_ready, 1)

                def take_ctx(b, s):
                    g, t = s // T, s % T
                    dve.wait_ge(recip_copied, STEPS * b + s + 1)
                    v.tensor_tensor(ctx_t[:, g, t * P:(t + 1) * P], ps_x[s % 2][:, 0:P], recip_b[s % 2][:, :],
                                    ALU.mult).then_inc(ctx_taken, 1)

                def make_mask(n):
                    dve.wait_ge(mask_landed, 16 * n + 16)
                    v.tensor_scalar(masked_add[:, :, :], mask_in[:, :, :], MASKED, None, ALU.mult).then_inc(mask_made, 1)

                make_mask(0)
                with dve.Fori(0, B) as b:
                    for t in (1, 3):
                        take_job(b, JOB_X + t, xt[:, t, :])
                    for t in (1, 3):
                        take_job(b, JOB_V + t, v_sb[:, t, :])
                    take_job(b, JOB_QK + 1, kt[0][:, :], bias=bk[:, 0:1])
                    norm = None
                    for t in range(UNITS + 8):
                        if t < UNITS:
                            bias_and_max(b, t)
                        if t - 3 >= 0 and t - 3 < UNITS and (t - 3) % 2:
                            take_turned(b, t - 3)
                        if t - 2 >= 0 and t - 2 < UNITS and (t - 2) % GH == GH - 1:
                            reciprocal(b, (t - 2) // GH)
                        for g in range(1, GROUPS):
                            if t == q_slot(g) + 1:
                                take_job(b, JOB_QK + 2 * g + 1, kt[g % 2][:, :], bias=bk[:, g:g + 1])
                        if t >= 8 and (t - 8) % GH == GH - 1:
                            take_ctx(b, (t - 8) // GH)
                        if t == 24:
                            dve.wait_ge(residual_made, b + 1)
                            norm = norm_steps(dve, v, b + 1)
                        if norm:
                            next(norm, None)
                        if t == UNITS - 2:
                            dve.wait_ge(bias_masked, STEPS * b + STEPS)
                            make_mask(b + 1)
                    dve.wait_ge(residual_made, b + 1)
                    for t in range(T):
                        i = (JOB_O + t) % 2
                        take_job(b, JOB_O + t, residual[:, t, :], add=residual[:, t, :]).then_inc(job_taken[i], 1)

            @block.scalar
            def _(act):
                def take_job(b, job, out, scale=1.0, bias=0.0):
                    i = job % 2
                    act.wait_ge(job_filled[i], NJ * b + job // 2 + 1)
                    nc.scalar.activation(out, ps_m[i][:, :], ACT.Identity, scale=scale, bias=bias).then_inc(job_taken[i], 1)

                def exponent(b, u):
                    s, h = u // GH, u % GH
                    act.wait_ge(scores_biased, UNITS * b + u + 1)
                    tile = probs[s % RING][:, h, :]
                    nc.scalar.activation(tile, tile, ACT.Exp, scale=-1.0, bias=neg_max[s % 2][:, h:h + 1],
                                         accum_out=sums[s % 2][:, h:h + 1]).then_inc(probs_ready, 1)

                def take_turned(b, u):
                    s, h = u // GH, u % GH
                    act.wait_ge(probs_turned, UNITS * b + u + 1 + RING * GH)
                    if h == 0:
                        act.wait_ge(ctx_ready, STEPS * b + s + 1)
                    nc.scalar.copy(probs_t[s % 2][:, h, :, :].rearrange("p t k -> p (t k)"),
                                   ps_p[u % 2][:, :]).then_inc(turned_taken[u % 2], 1)

                def copy_recip(b, s):
                    act.wait_ge(recip_spread, STEPS * b + s + 1)
                    act.wait_ge(ctx_taken, STEPS * b + s + 1)
                    nc.scalar.copy(recip_b[s % 2][:, :], ps_x[s % 2][:, P:2 * P]).then_inc(recip_copied, 1)

                act.wait_ge(consts, 3)
                with act.Fori(0, B) as b:
                    for t in (0, 2):
                        take_job(b, JOB_X + t, xt[:, t, :])
                    for t in (0, 2):
                        take_job(b, JOB_V + t, v_sb[:, t, :])
                    take_job(b, JOB_QK, qt[0][:, :], scale=DH ** -0.5, bias=bq[:, 0:1])
                    for t in range(UNITS + 8):
                        if t < UNITS:
                            exponent(b, t)
                        if t - 3 >= 0 and t - 3 < UNITS and (t - 3) % 2 == 0:
                            take_turned(b, t - 3)
                        for g in range(1, GROUPS):
                            if t == q_slot(g) + 1:
                                take_job(b, JOB_QK + 2 * g, qt[g % 2][:, :], scale=DH ** -0.5, bias=bq[:, g:g + 1])
                        if t >= 8 and (t - 8) % GH == GH - 1:
                            copy_recip(b, (t - 8) // GH)
                    for i in range(2):
                        act.wait_ge(job_taken[i], START + NJ * b + NJ)
                    act.dma_start(x1_dram[b].rearrange("(p t) d -> p t d", t=T), residual[:, :, :]).then_inc(x1_stored, 16)

            @block.tensor
            def _(pe):
                def job(b, n, products):
                    i = n % 2
                    pe.wait_ge(job_taken[i], START + NJ * b + n // 2)
                    for k, (lhs, rhs) in enumerate(products):
                        last = nc.tensor.matmul(ps_m[i][:, :], lhs, rhs, start=(k == 0), stop=(k == len(products) - 1))
                    last.then_inc(job_filled[i], 1)

                def project_qk(b, g):
                    cols = slice(g * P, (g + 1) * P)
                    job(b, JOB_QK + 2 * g, [(wq[:, t, cols], xt[:, t, :]) for t in range(DT)])
                    job(b, JOB_QK + 2 * g + 1, [(wk[:, t, cols], xt[:, t, :]) for t in range(DT)])

                def scores(b, u):
                    s, h = u // GH, u % GH
                    g, t = s // T, s % T
                    if s % T == 0 and h == 0:
                        for i in range(2):
                            pe.wait_ge(job_taken[i], START + NJ * b + (JOB_QK + 2 * g) // 2 + 1)
                    if u >= 2:
                        pe.wait_ge(scores_biased, UNITS * b + u - 1)
                    rows = slice(h * DH, (h + 1) * DH)
                    nc.tensor.matmul(ps_s[u % 2][:, :], qt[g % 2][rows, t * P:(t + 1) * P], kt[g % 2][rows, :],
                                     start=True, stop=True).then_inc(scores_ready, 1)

                def turn(b, u):
                    s, h = u // GH, u % GH
                    pe.wait_ge(probs_ready, UNITS * b + u + 1)
                    pe.wait_ge(turned_taken[u % 2], START + (UNITS // 2) * b + u // 2)
                    for t in range(T):
                        last = nc.tensor.transpose(ps_p[u % 2][:, t * P:(t + 1) * P],
                                                   probs[s % RING][:, h, t:S:T], ident[:, :])
                    last.then_inc(probs_turned, 1)

                def context(b, s):
                    g = s // T
                    for i in range(2):
                        pe.wait_ge(turned_taken[i], START + (UNITS // 2) * b + 2 * s + 2)
                    pe.wait_ge(ctx_taken, STEPS * b + s + 1)
                    for t in range(T):
                        for h in range(GH):
                            col = g * P + h * DH
                            last = nc.tensor.matmul(ps_x[s % 2][h * DH:(h + 1) * DH, 0:P], v_sb[:, t, col:col + DH],
                                                    probs_t[s % 2][:, h, t, :], start=(t == 0), stop=(t == T - 1))
                    last.then_inc(ctx_ready, 1)
                    pe.wait_ge(recip_ready, STEPS * b + s + 1)
                    for h in range(GH):
                        last = nc.tensor.matmul(ps_x[s % 2][h * DH:(h + 1) * DH, P:2 * P],
                                                recip[s % 2][:, h:h + 1].to_broadcast([P, DH]), ident[:, :],
                                                start=True, stop=True)
                    last.then_inc(recip_spread, 1)

                pe.wait_ge(weights_in, 16 * 7)
                pe.wait_ge(ident_made, 1)
                pe.sem_inc(probs_turned, RING * GH)
                pe.sem_inc(ctx_ready, 2)
                with pe.Fori(0, B) as b:
                    pe.wait_ge(xn_ready, b + 1)
                    for t in range(DT):
                        i = t % 2
                        pe.wait_ge(job_taken[i], START + NJ * b + t // 2)
                        for j in range(T):
                            last = nc.tensor.transpose(ps_m[i][:, j * P:(j + 1) * P], xn[:, j, t * P:(t + 1) * P], ident[:, :])
                        last.then_inc(job_filled[i], 1)
                    for i in range(2):
                        pe.wait_ge(job_taken[i], START + NJ * b + 2)
                    for j in range(T):
                        job(b, JOB_V + j, [(xt[:, t, j * P:(j + 1) * P], wv[:, t, :]) for t in range(DT)])
                    project_qk(b, 0)
                    for t in range(UNITS + 4):
                        for g in range(1, GROUPS):
                            if t == q_slot(g):
                                project_qk(b, g)
                        if t < UNITS:
                            scores(b, t)
                        if 0 <= t - 2 < UNITS:
                            turn(b, t - 2)
                        if t >= 4 and (t - 4) % GH == GH - 1:
                            context(b, (t - 4) // GH)
                    pe.wait_ge(ctx_taken, STEPS * b + STEPS + 2)
                    for j in range(T):
                        job(b, JOB_O + j, [(ctx_t[:, g, j * P:(j + 1) * P], wo[:, g, :]) for g in range(GROUPS)])


def feed_forward(nc, a, x1_dram, y_dram):
    B = a["x"].shape[0]
    with ExitStack() as ctx:
        def sb(name, shape, dt=F32):
            return ctx.enter_context(nc.sbuf_tensor("ff_" + name, shape, dt))

        def sem(name):
            return ctx.enter_context(nc.semaphore("ff_" + name))

        def bank(name):
            return ctx.enter_context(nc.psum_tensor("ff_" + name, [P, 512], F32))

        ident = sb("ident", [P, P])
        w1, w2 = sb("w1", [P, DT, FF]), sb("w2", [P, FT, D])
        b1 = sb("b1", [P, FT])
        b2, g2, beta2 = sb("b2", [P, D]), sb("g2", [P, DT]), sb("beta2", [P, DT])
        down, down_t, down_b = sb("down", [P, D]), sb("down_t", [P, DT, ADP]), sb("down_b", [P, 1])
        up, up_t, up_b = sb("up", [P, DT, ADP]), sb("up_t", [P, D]), sb("up_b", [P, D])
        experts, experts_t = sb("experts", [P, EXPERTS, ADP]), sb("experts_t", [P, EXPERTS, ADP])
        gamma, beta = sb("gamma", [P, D]), sb("beta", [P, D])
        ids, id_col = sb("ids", [P, EXPERTS]), sb("id_col", [EXPERTS, 1])
        expert_b, expert_e = sb("expert_b", [EXPERTS, ADP]), sb("expert_e", [EXPERTS, ADP])
        dom_i, dom, dom_in = sb("dom_i", [P, B], I32), sb("dom", [P, B]), sb("dom_in", [P, B])
        valid = sb("valid", [P, B])
        pick = sb("pick", [P, B, EXPERTS + 1])
        pick_e, pick_b = sb("pick_e", [EXPERTS, B]), sb("pick_b", [EXPERTS, B])
        shift_all = sb("shift_all", [P, B])
        pick_now, shift_now = sb("pick_now", [P, EXPERTS + 1]), sb("shift_now", [P, 1])
        expert = [sb(f"expert{i}", [P, ADP]) for i in range(2)]
        power, eps = sb("power", [P, T]), sb("eps", [P, T])
        x1 = sb("x1", [P, T, D])
        hidden = sb("hidden", [P, T, D])
        stats, moments, rstd = sb("stats", [P, T, 6]), sb("moments", [P, T, 2]), sb("rstd", [P, T])
        ht = sb("ht", [P, DT, S])
        act_t = sb("act_t", [P, FT, S])
        x2 = sb("x2", [P, T, D])
        x2t = sb("x2t", [P, DT, S])
        low, mixed = sb("low", [P, S]), sb("mixed", [P, S])
        y = sb("y", [P, T, D])
        stats_y, moments_y, rstd_y = sb("stats_y", [P, T, 6]), sb("moments_y", [P, T, 2]), sb("rstd_y", [P, T])
        ps = [bank(f"ps{i}") for i in range(4)]

        weights_in, zeroed, ident_made = sem("weights_in"), sem("zeroed"), sem("ident_made")
        pick_chain, picked, consts = sem("pick_chain"), sem("picked"), sem("consts")
        setup_mm, setup_taken = sem("setup_mm"), sem("setup_taken")
        x1_landed, norm_chain, rstd_made, hidden_ready = sem("x1_landed"), sem("norm_chain"), sem("rstd_made"), sem("hidden_ready")
        filled = [sem(f"filled{i}") for i in range(4)]
        taken = [sem(f"taken{i}") for i in range(4)]
        x1_base, expert_chain = sem("x1_base"), sem("expert_chain")
        x2_base, y_chain, rstd_y_made, y_ready, y_stored = sem("x2_base"), sem("y_chain"), sem("rstd_y_made"), sem("y_ready"), sem("y_stored")
        passed = sem("passed")
        eps_chain, gamma_done = sem("eps_chain"), sem("gamma_done")

        JOB_H, JOB_1, JOB_2, JOB_X = 0, DT, DT + FT, DT + FT + T
        JOB_DOWN = JOB_X + DT
        JOB_MIX, JOB_UP = JOB_DOWN + 1, JOB_DOWN + 2
        JOBS = JOB_UP + T
        JOBS += -JOBS % 4
        NJ = JOBS // 4
        EMPTY = range(JOB_UP + T, JOBS)
        NORM = 3 * T
        Y_NORM = 3 * T
        WEIGHTS = 16

        with nc.Block() as block:
            @block.sync
            def _(sp):
                for counted in [*taken, y_stored, x2_base]:
                    sp.sem_inc(counted, START)
                def load(out, array, **how):
                    sp.dma_start(out, array, **how).then_inc(weights_in, 16)

                sp.dma_start(x1[:, :, :], x1_dram[0].rearrange("(p t) d -> p t d", t=T)).then_inc(x1_landed, 16)
                load(down[:, :], a["L2_cond_down_W"])
                load(up[:, :, :], a["L2_cond_up_W"].rearrange("(t p) n -> p t n", p=P))
                load(experts[:, :, :], a["L2_cond_expert_W"].rearrange("e o i -> o e i"))
                load(dom_i[:, :], a["itok_B_0_15"].partition_broadcast(P))
                load(ids[:, :], a["expert_ids"].partition_broadcast(P))
                load(id_col[:, :], a["expert_ids"].rearrange("(e o) -> e o", o=1))
                load(expert_b[:, :], a["L2_cond_expert_b"])
                load(expert_e[:, :], a["L2_cond_domain_emb"])
                load(w1[:, :, :], a["L1_cond_W1"].rearrange("(t p) n -> p t n", p=P))
                load(w2[:, :, :], a["L1_cond_W2"].rearrange("(t p) n -> p t n", p=P))
                for out, n in ((b1, "L1_cond_b1"), (g2, "L1_cond_g2"), (beta2, "L1_cond_beta2"), (down_b, "L2_cond_down_b")):
                    load(out[:, :], a[n].rearrange("(t p) -> p t", p=P), allow_slow_non_contiguous=True)
                for out, n in ((b2, "L1_cond_b2"), (up_b, "L2_cond_up_b")):
                    load(out[:, :], a[n].partition_broadcast(P))
                sp.dma_start(gamma[:, :], a["L2_cond_ln_gamma"].partition_broadcast(P)).then_inc(consts, 16)
                sp.dma_start(beta[:, :], a["L2_cond_ln_beta"].partition_broadcast(P)).then_inc(consts, 16)
                with sp.Fori(0, B) as b:
                    following = sp.snap((b + 1) % B)
                    sp.wait_ge(x1_base, b + 1)
                    apart(sp, passed)
                    sp.dma_start(x1[:, :, :], x1_dram[following].rearrange("(p t) d -> p t d", t=T)).then_inc(x1_landed, 16)
                    sp.wait_ge(y_ready, b + 1)
                    apart(sp, passed)
                    sp.dma_start(y_dram[b].rearrange("(p t) d -> p t d", t=T), y[:, :, :]).then_inc(y_stored, 16)
                sp.wait_ge(y_stored, START + 16 * B)
                sp.wait_ge(x1_landed, 16 * B + 16)

            @block.gpsimd
            def _(pool):
                g_ = nc.gpsimd
                identity(nc, pool, ident, zeroed).then_inc(ident_made, 1)
                g_.memset(eps[:, :], EPS).then_inc(ident_made, 1)
                pool.wait_ge(ident_made, 2)
                g_.memset(power[:, :], -0.5).then_inc(eps_chain, 1)

                def inverse_deviation(n, out, source, ready, chain_before, made):
                    pool.wait_ge(ready, chain_before)
                    pool.wait_ge(eps_chain, n)
                    g_.tensor_tensor(out[:, :], source[:, :, 1], eps[:, :], ALU.add).then_inc(eps_chain, 1)
                    pool.wait_ge(eps_chain, n + 1)
                    g_.tensor_tensor(out[:, :], out[:, :], power[:, :], ALU.pow).then_inc(made, 1)

                def base_of_x2(b):
                    pool.wait_ge(norm_chain, NORM * b + NORM)
                    pool.wait_ge(x2_base, START + b)
                    pool.wait_ge(taken[(JOB_UP + T - 1) % 4], START + NJ * b)
                    g_.tensor_tensor(x2[:, :, :], x1[:, :, :], b2[:, :].unsqueeze(1).to_broadcast([P, T, D]),
                                     ALU.add).then_inc(x1_base, 1)

                pool.wait_ge(weights_in, 16 * WEIGHTS)
                inverse_deviation(1, rstd, moments, norm_chain, 2 * T, rstd_made)
                with pool.Fori(0, B) as b:
                    base_of_x2(b)
                    inverse_deviation(2 * b + 2, rstd, moments, norm_chain, NORM * b + NORM + 2 * T, rstd_made)
                    pool.wait_ge(filled[(JOB_X + DT - 1) % 4], NJ * b + (JOB_X + DT - 1) // 4 + 1)
                    g_.tensor_tensor(x2[:, :, :], x2[:, :, :], up_b[:, :].unsqueeze(1).to_broadcast([P, T, D]),
                                     ALU.add).then_inc(x2_base, 1)
                    inverse_deviation(2 * b + 3, rstd_y, moments_y, y_chain, Y_NORM * b + 2 * T, rstd_y_made)
                    pool.wait_ge(y_chain, Y_NORM * b + Y_NORM)
                    pool.wait_ge(consts, 32)
                    g_.tensor_tensor(y[:, :, :], y[:, :, :], gamma[:, :].unsqueeze(1).to_broadcast([P, T, D]),
                                     ALU.mult).then_inc(gamma_done, 1)
                    pool.wait_ge(gamma_done, b + 1)
                    g_.tensor_tensor(y[:, :, :], y[:, :, :], beta[:, :].unsqueeze(1).to_broadcast([P, T, D]),
                                     ALU.add).then_inc(y_ready, 1)

            def statistics(dve, v, source, stats, moments, chain, base):
                for t in range(T):
                    v.bn_stats(stats[:, t, :], source[:, t, :]).then_inc(chain, 1)
                dve.wait_ge(chain, base + T)
                apart(dve, passed)
                for t in range(T):
                    v.bn_aggr(moments[:, t, :], stats[:, t, :]).then_inc(chain, 1)

            def normalise(dve, v, out, source, moments, rstd, chain):
                for t in range(T):
                    v.tensor_scalar(out[:, t, :], source[:, t, :], moments[:, t, 0:1], rstd[:, t:t + 1],
                                    ALU.subtract, ALU.mult).then_inc(chain, 1)

            @block.vector
            def _(dve):
                v = nc.vector
                done = [0]

                def then(ins):
                    ins.then_inc(pick_chain, 1)
                    done[0] += 1
                    dve.wait_ge(pick_chain, done[0])

                dve.wait_ge(weights_in, 16 * WEIGHTS)
                dve.wait_ge(ident_made, 1)
                then(v.tensor_copy(dom_in[:, :], dom_i[:, :]))
                then(v.tensor_scalar(dom[:, :], dom_in[:, :], 0.0, float(EXPERTS - 1), ALU.max, ALU.min))
                then(v.tensor_tensor(valid[:, :], dom[:, :], dom_in[:, :], ALU.is_equal))
                for n in range(B):
                    then(v.tensor_scalar(pick[:, n, 0:EXPERTS], ids[:, :], dom[:, n:n + 1], valid[:, n:n + 1],
                                         ALU.is_equal, ALU.mult))
                then(v.tensor_scalar(pick[:, :, EXPERTS], valid[:, :], -1.0, 1.0, ALU.mult, ALU.add))
                then(v.tensor_scalar(pick_e[:, :], dom[0:EXPERTS, :], id_col[:, :], None, ALU.is_equal))
                then(v.tensor_tensor(pick_b[:, :], pick_e[:, :], valid[0:EXPERTS, :], ALU.mult))
                v.memset(low[:, 0:1], 0.0).then_inc(picked, 1)
                for k in range(6):
                    out = [down_t[:, :, :], up_t[:, :].rearrange("p (t n) -> p t n", t=DT)] + \
                          [experts_t[:, 4 * i:4 * i + 4, :] for i in range(4)]
                    dve.wait_ge(setup_mm, k + 1)
                    v.tensor_copy(out[k], ps[k % 4][:, :].rearrange("p (t n) -> p t n", t=4)).then_inc(setup_taken, 1)
                dve.wait_ge(setup_mm, 7)
                v.tensor_copy(shift_all[:, :], ps[2][:, 0:B]).then_inc(setup_taken, 1)
                dve.wait_ge(setup_taken, 7)

                dve.wait_ge(x1_landed, 16)
                statistics(dve, v, x1, stats, moments, norm_chain, 0)
                dve.wait_ge(rstd_made, 1)
                normalise(dve, v, hidden, x1, moments, rstd, norm_chain)
                with dve.Fori(0, B) as b:
                    def take(job):
                        dve.wait_ge(filled[job % 4], NJ * b + job // 4 + 1)
                        return ps[job % 4][:, :]

                    for t in range(1, DT, 2):
                        v.tensor_scalar(ht[:, t, :], take(JOB_H + t), g2[:, t:t + 1], beta2[:, t:t + 1],
                                        ALU.mult, ALU.add).then_inc(taken[(JOB_H + t) % 4], 1)
                    E = (EXPERTS + 3) * b
                    v.tensor_copy(pick_now[:, :], pick[:, bass.ds(b, 1), :].rearrange("p o e -> p (o e)")).then_inc(expert_chain, 1)
                    v.tensor_copy(shift_now[:, :], shift_all[:, bass.ds(b, 1)]).then_inc(expert_chain, 1)
                    dve.wait_ge(expert_chain, E + 2)
                    v.tensor_scalar(expert[0][:, :], ident[:, :], pick_now[:, EXPERTS:EXPERTS + 1], None,
                                    ALU.mult).then_inc(expert_chain, 1)
                    for e in range(EXPERTS):
                        dve.wait_ge(expert_chain, E + 3 + e)
                        v.scalar_tensor_tensor(expert[(e + 1) % 2][:, :], experts_t[:, e, :], pick_now[:, e:e + 1],
                                               expert[e % 2][:, :], ALU.mult, ALU.add).then_inc(expert_chain, 1)
                    dve.wait_ge(x1_landed, 16 * b + 32)
                    statistics(dve, v, x1, stats, moments, norm_chain, NORM * b + NORM)
                    dve.wait_ge(rstd_made, b + 2)
                    for i in range(4):
                        dve.wait_ge(filled[i], NJ * b + 1)
                    normalise(dve, v, hidden, x1, moments, rstd, norm_chain)
                    dve.wait_ge(x1_base, b + 1)
                    for t in range(T):
                        v.tensor_tensor(x2[:, t, :], take(JOB_2 + t), x2[:, t, :], ALU.add).then_inc(taken[(JOB_2 + t) % 4], 1)
                    for t in range(1, DT, 2):
                        v.tensor_copy(x2t[:, t, :], take(JOB_X + t)).then_inc(taken[(JOB_X + t) % 4], 1)
                    v.tensor_scalar(mixed[:, :], take(JOB_MIX), shift_now[:, :], None, ALU.add).then_inc(taken[JOB_MIX % 4], 1)
                    dve.wait_ge(x2_base, START + b + 1)
                    dve.wait_ge(y_stored, START + 16 * b)
                    for t in range(T):
                        v.tensor_tensor(y[:, t, :], take(JOB_UP + t), x2[:, t, :], ALU.add).then_inc(taken[(JOB_UP + t) % 4], 1)
                    for t in range(T):
                        dve.wait_ge(taken[(JOB_UP + t) % 4], START + NJ * b + (JOB_UP + t) // 4 + 1)
                    statistics(dve, v, y, stats_y, moments_y, y_chain, Y_NORM * b)
                    dve.wait_ge(rstd_y_made, b + 1)
                    normalise(dve, v, y, y, moments_y, rstd_y, y_chain)
                    for job in EMPTY:
                        dve.wait_ge(filled[job % 4], NJ * b + job // 4 + 1)
                        dve.sem_inc(taken[job % 4], 1)

            @block.scalar
            def _(act):
                act.wait_ge(weights_in, 16 * WEIGHTS)
                with act.Fori(0, B) as b:
                    def take(job):
                        act.wait_ge(filled[job % 4], NJ * b + job // 4 + 1)
                        return ps[job % 4][:, :]

                    for t in range(0, DT, 2):
                        nc.scalar.activation(ht[:, t, :], take(JOB_H + t), ACT.Identity, scale=g2[:, t:t + 1],
                                             bias=beta2[:, t:t + 1]).then_inc(taken[(JOB_H + t) % 4], 1)
                    for t in range(FT):
                        nc.scalar.activation(act_t[:, t, :], take(JOB_1 + t), ACT.Gelu_apprx_sigmoid,
                                             bias=b1[:, t:t + 1]).then_inc(taken[(JOB_1 + t) % 4], 1)
                    for t in range(0, DT, 2):
                        nc.scalar.copy(x2t[:, t, :], take(JOB_X + t)).then_inc(taken[(JOB_X + t) % 4], 1)
                    nc.scalar.activation(low[:, :], take(JOB_DOWN), ACT.Gelu,
                                         bias=down_b[:, 0:1]).then_inc(taken[JOB_DOWN % 4], 1)

            @block.tensor
            def _(pe):
                pe.wait_ge(weights_in, 16 * WEIGHTS)
                pe.wait_ge(ident_made, 1)
                for k in range(6):
                    if k >= 4:
                        pe.wait_ge(setup_taken, k - 3)
                    for i in range(4):
                        source = down[:, i * P:(i + 1) * P] if k == 0 else up[:, i, :] if k == 1 else experts[:, 4 * (k - 2) + i, :]
                        last = nc.tensor.transpose(ps[k % 4][:, i * P:(i + 1) * P], source, ident[:, :])
                    last.then_inc(setup_mm, 1)
                pe.wait_ge(picked, 1)
                pe.wait_ge(setup_taken, 3)
                nc.tensor.matmul(ps[2][:, 0:B], expert_b[:, :], pick_b[:, :], start=True, stop=False)
                nc.tensor.matmul(ps[2][:, 0:B], expert_e[:, :], pick_e[:, :], start=False, stop=True).then_inc(setup_mm, 1)
                pe.wait_ge(setup_taken, 7)
                pe.wait_ge(norm_chain, NORM)
                with pe.Fori(0, B) as b:
                    def free(job):
                        pe.wait_ge(taken[job % 4], START + NJ * b + job // 4)

                    def until_taken(job, n):
                        for k in range(max(job, job + n - 4), job + n):
                            pe.wait_ge(taken[k % 4], START + NJ * b + k // 4 + 1)

                    def product(job, pairs):
                        free(job)
                        for k, (lhs, rhs) in enumerate(pairs):
                            last = nc.tensor.matmul(ps[job % 4][:, :], lhs, rhs, start=(k == 0), stop=(k == len(pairs) - 1))
                        last.then_inc(filled[job % 4], 1)

                    def turn(job, source):
                        for t in range(DT):
                            free(job + t)
                            for j in range(T):
                                last = nc.tensor.transpose(ps[(job + t) % 4][:, j * P:(j + 1) * P],
                                                           source[:, j, t * P:(t + 1) * P], ident[:, :])
                            last.then_inc(filled[(job + t) % 4], 1)

                    pe.wait_ge(norm_chain, NORM * b + NORM)
                    turn(JOB_H, hidden)
                    until_taken(JOB_H, DT)
                    for f in range(FT):
                        product(JOB_1 + f, [(w1[:, t, f * P:(f + 1) * P], ht[:, t, :]) for t in range(DT)])
                    until_taken(JOB_1, FT)
                    for j in range(T):
                        product(JOB_2 + j, [(act_t[:, f, j * P:(j + 1) * P], w2[:, f, :]) for f in range(FT)])
                    until_taken(JOB_2, T)
                    turn(JOB_X, x2)
                    until_taken(JOB_X, DT)
                    product(JOB_DOWN, [(down_t[:, t, :], x2t[:, t, :]) for t in range(DT)])
                    until_taken(JOB_DOWN, 1)
                    pe.wait_ge(expert_chain, (EXPERTS + 3) * b + EXPERTS + 3)
                    product(JOB_MIX, [(expert[EXPERTS % 2][:, :], low[:, :])])
                    until_taken(JOB_MIX, 1)
                    for j in range(T):
                        product(JOB_UP + j, [(mixed[:, j * P:(j + 1) * P], up_t[:, :])])
                    for job in EMPTY:
                        free(job)
                        pe.sem_inc(filled[job % 4], 1)


def stencil(nc, a, y_dram, edge_dram, ghost_dram, out_dram):
    B = a["x"].shape[0]
    W = D + 2
    with ExitStack() as ctx:
        def sb(name, shape, dt=F32):
            return ctx.enter_context(nc.sbuf_tensor("st_" + name, shape, dt))

        def sem(name):
            return ctx.enter_context(nc.semaphore("st_" + name))

        raw = [sb(f"raw{i}", [P, T, D]) for i in range(4)]
        grid_q = sb("grid_q", [P, T, D])
        grid_up, grid_dn = sb("grid_up", [P, T, D]), sb("grid_dn", [P, T, D])
        grid_rt, grid_lf = sb("grid_rt", [P, T, D]), sb("grid_lf", [P, T, D])
        grid_mid = raw[0]
        edges = sb("edges", [P, 3, 2 * T])
        dts, dt_now = sb("dts", [P, B]), sb("dt_now", [P, 1])
        f = sb("f", [P, T, D])
        q = sb("q", [P, T, W])
        slope = sb("slope", [P, T, D])
        up, dn = sb("up", [P, T + 1, D]), sb("dn", [P, T + 1, D])
        cols = sb("cols", [P, T, 2, W])
        side = sb("side", [P, T, D])
        total = sb("total", [P, T, D])
        chunk = 2 * D // P
        near = sb("near", [P, 2 * T, chunk])
        near_p = sb("near_p", [P, 2 * T, chunk])
        ghost = sb("ghost", [P, chunk])
        col_p = sb("col_p", [P, T, 2, T])

        grids_in, small_in, chain, grids_made = sem("grids_in"), sem("small_in"), sem("chain"), sem("grids_made")
        f_landed, rows_made, rows_out, near_in = sem("f_landed"), sem("rows_made"), sem("rows_out"), sem("near_in")
        ghost_made, ghost_out, rows_in, shifted = sem("ghost_made"), sem("ghost_out"), sem("rows_in"), sem("shifted")
        cols_made, side_made, batch_done, stored = sem("cols_made"), sem("side_made"), sem("batch_done"), sem("stored")
        dve_chain, pool_chain, edge_cols = sem("dve_chain"), sem("pool_chain"), sem("edge_cols")
        passed = sem("passed")
        LINKS = 24

        with nc.Block() as block:
            @block.sync
            def _(sp):
                for counted in [batch_done, stored, dve_chain]:
                    sp.sem_inc(counted, START)
                for k in range(2):
                    sp.dma_start(raw[k][:, :, :], a["L3_cond_A_grid"][k].rearrange("(p t) d -> p t d", t=T)).then_inc(grids_in, 16)
                    sp.dma_start(raw[2 + k][:, :, :], a["L3_cond_B_grid"][k].rearrange("(p t) d -> p t d", t=T)).then_inc(grids_in, 16)
                sp.dma_start(grid_q[:, :, :], a["L3_cond_B_grid"][2].rearrange("(p t) d -> p t d", t=T)).then_inc(grids_in, 16)
                sp.dma_start(edges[:, :, :].rearrange("p a b -> p (a b)"), a["edge_weights"].partition_broadcast(P)).then_inc(small_in, 16)
                sp.dma_start(dts[:, :], a["condB_dt"].partition_broadcast(P)).then_inc(small_in, 16)
                with sp.Fori(0, B) as b:
                    sp.wait_ge(batch_done, START + b)
                    apart(sp, passed)
                    sp.dma_start(f[:, :, :], y_dram[b].rearrange("(p t) d -> p t d", t=T)).then_inc(f_landed, 16)
                    sp.wait_ge(rows_made, b + 1)
                    sp.dma_start(up[0:P - 1, T, :], up[1:P, 0, :]).then_inc(shifted, 16)
                    sp.dma_start(dn[1:P, 0, :], dn[0:P - 1, T, :]).then_inc(shifted, 16)
                    sp.dma_start(edge_dram[0, 0:T], dn[0:1, 1:T + 1, :]).then_inc(rows_out, 16)
                    sp.dma_start(edge_dram[0, T:2 * T], up[0:1, 0:T, :]).then_inc(rows_out, 16)
                    for t in range(T):
                        sp.dma_start(edge_dram[1, t:t + 1], up[P - 1:P, T - 1 - t:T - t, :]).then_inc(rows_out, 16)
                        sp.dma_start(edge_dram[1, T + t:T + t + 1], dn[P - 1:P, T - t:T - t + 1, :]).then_inc(rows_out, 16)
                    sp.wait_ge(rows_out, 160 * b + 160)
                    for k in range(2):
                        sp.dma_start(near[k * P // 2:(k + 1) * P // 2, :, :],
                                     edge_dram[k].rearrange("r (c i) -> c r i", i=chunk)).then_inc(near_in, 16)
                    sp.wait_ge(ghost_made, b + 1)
                    sp.dma_start(ghost_dram.rearrange("k (c i) -> (k c) i", i=chunk), ghost[:, :]).then_inc(ghost_out, 16)
                    sp.wait_ge(ghost_out, 16 * b + 16)
                    sp.dma_start(dn[0:1, 0, :], ghost_dram[0:1]).then_inc(rows_in, 16)
                    sp.dma_start(up[P - 1:P, T, :], ghost_dram[1:2]).then_inc(rows_in, 16)
                    sp.wait_ge(batch_done, START + b + 1)
                    apart(sp, passed)
                    sp.dma_start(out_dram[b].rearrange("(p t) d -> p t d", t=T), total[:, :, :]).then_inc(stored, 16)
                sp.wait_ge(stored, START + 16 * B)

            @block.gpsimd
            def _(pool):
                g_ = nc.gpsimd
                pool.wait_ge(grids_made, 1)
                with pool.Fori(0, B) as b:
                    pool.wait_ge(f_landed, 16 * b + 16)
                    pool.wait_ge(batch_done, START + b)
                    g_.tensor_tensor(cols[:, :, 0, 1:D + 1], grid_rt[:, :, :], f[:, :, :], ALU.mult).then_inc(cols_made, 1)
                    g_.tensor_tensor(cols[:, :, 1, 1:D + 1], grid_lf[:, :, :], f[:, :, :], ALU.mult).then_inc(cols_made, 1)
                    g_.tensor_tensor(side[:, :, :], grid_mid[:, :, :], f[:, :, :], ALU.mult).then_inc(cols_made, 1)
                    pool.wait_ge(cols_made, 3 * b + 3)
                    pool.wait_ge(edge_cols, 2 * b + 2)
                    g_.tensor_tensor(side[:, :, :], cols[:, :, 0, 2:W], side[:, :, :], ALU.subtract).then_inc(pool_chain, 1)
                    pool.wait_ge(pool_chain, b + 1)
                    g_.tensor_tensor(side[:, :, :], cols[:, :, 1, 0:D], side[:, :, :], ALU.add).then_inc(side_made, 1)

            @block.vector
            def _(dve):
                v = nc.vector
                done = [0]

                def then(ins):
                    ins.then_inc(chain, 1)
                    done[0] += 1
                    dve.wait_ge(chain, done[0])

                dve.wait_ge(grids_in, 80)
                dve.wait_ge(small_in, 32)
                for k, (minus, plus) in enumerate(((grid_up, grid_dn), (grid_rt, grid_lf))):
                    for out, op in ((minus, ALU.subtract), (plus, ALU.add)):
                        then(v.tensor_tensor(out[:, :, :], raw[2 + k][:, :, :], raw[k][:, :, :], op))
                        then(v.tensor_scalar(out[:, :, :], out[:, :, :], 0.5, None, ALU.mult))
                then(v.tensor_tensor(grid_mid[:, :, :], raw[2][:, :, :], raw[3][:, :, :], ALU.add))
                then(v.tensor_scalar(grid_q[:, :, :], grid_q[:, :, :], 0.25, None, ALU.mult))
                v.tensor_copy(dt_now[:, :], dts[:, 0:1]).then_inc(grids_made, 1)
                dve.wait_ge(grids_made, 1)

                with dve.Fori(0, B) as b:
                    k = [0]

                    def link(ins):
                        ins.then_inc(dve_chain, 1)
                        k[0] += 1

                    def ready():
                        dve.wait_ge(dve_chain, START + LINKS * b + k[0])

                    dve.wait_ge(f_landed, 16 * b + 16)
                    dve.wait_ge(stored, START + 16 * b)
                    ready()
                    link(v.tensor_copy(dt_now[:, :], dts[:, bass.ds(b, 1)]))
                    link(v.tensor_tensor(q[:, :, 1:D + 1], grid_q[:, :, :], f[:, :, :], ALU.mult))
                    link(v.tensor_tensor(up[:, 0:T, :], grid_up[:, :, :], f[:, :, :], ALU.mult))
                    link(v.tensor_tensor(dn[:, 1:T + 1, :], grid_dn[:, :, :], f[:, :, :], ALU.mult))
                    ready()
                    for out, x0, x1, x2 in ((0, 1, 2, 3), (D + 1, D, D - 1, D - 2)):
                        link(v.tensor_tensor(q[:, :, out], q[:, :, x0], q[:, :, x1], ALU.subtract))
                        ready()
                        link(v.scalar_tensor_tensor(q[:, :, out], q[:, :, out], 3.0, q[:, :, x2], ALU.mult, ALU.add))
                        ready()
                    link(v.tensor_tensor(slope[:, :, :], q[:, :, 2:W], q[:, :, 0:D], ALU.subtract))
                    ready()
                    link(v.tensor_tensor(up[:, 0:T, :], up[:, 0:T, :], slope[:, :, :], ALU.add))
                    link(v.tensor_tensor(dn[:, 1:T + 1, :], dn[:, 1:T + 1, :], slope[:, :, :], ALU.subtract))
                    ready()
                    v.sem_inc(rows_made, 1)
                    dve.wait_ge(cols_made, 3 * b + 2)
                    for c, (out, first) in enumerate(((0, 1), (D + 1, D + 1 - T))):
                        link(v.tensor_tensor(col_p[:, :, :, :], cols[:, :, :, first:first + T],
                                             edges[:, c, :].rearrange("p (a k) -> p a k", a=2).unsqueeze(1).to_broadcast([P, T, 2, T]),
                                             ALU.mult))
                        ready()
                        v.tensor_reduce(cols[:, :, 1 - c, out], col_p[:, :, :, :], mybir.AxisListType.XY,
                                        ALU.add).then_inc(edge_cols, 1)
                        dve.wait_ge(edge_cols, 2 * b + c + 1)
                    dve.wait_ge(near_in, 32 * b + 32)
                    link(v.tensor_tensor(near_p[:, :, :], near[:, :, :],
                                         edges[:, 2, :].unsqueeze(2).to_broadcast([P, 2 * T, chunk]), ALU.mult))
                    ready()
                    v.tensor_reduce(ghost[:, :], near_p[:, :, :].rearrange("p r i -> p i r"), mybir.AxisListType.X,
                                    ALU.add).then_inc(ghost_made, 1)
                    dve.wait_ge(shifted, 32 * b + 32)
                    dve.wait_ge(rows_in, 32 * b + 32)
                    link(v.tensor_tensor(total[:, :, :], up[:, 1:T + 1, :], dn[:, 0:T, :], ALU.add))
                    ready()
                    dve.wait_ge(side_made, b + 1)
                    link(v.tensor_tensor(total[:, :, :], total[:, :, :], side[:, :, :], ALU.add))
                    ready()
                    link(v.scalar_tensor_tensor(total[:, :, :], total[:, :, :], dt_now[:, :], f[:, :, :], ALU.mult, ALU.add))
                    ready()
                    while k[0] < LINKS - 1:
                        dve.sem_inc(dve_chain, 1)
                        k[0] += 1
                    v.tensor_scalar(total[:, :, :], total[:, :, :], 0.0, None, ALU.max).then_inc(batch_done, 1)
                    dve.wait_ge(batch_done, START + b + 1)
                    dve.sem_inc(dve_chain, 1)


_INS = ['x', 'condB_theta', 'condB_phi', 'itok_B_34_63', 'fside_Bx16xSxS_0', 'itok_B_0_15', 'condB_dt',
        'mask_Bx1xSxS_bk0', 'L1_cond_W_ada', 'L1_cond_b_ada', 'L1_cond_Wq', 'L1_cond_bq', 'L1_cond_Wk',
        'L1_cond_bk', 'L1_cond_Wv', 'L1_cond_bv', 'L1_cond_Wo', 'L1_cond_bo', 'L1_cond_W1', 'L1_cond_b1',
        'L1_cond_W2', 'L1_cond_b2', 'L1_cond_g2', 'L1_cond_beta2', 'L2_cond_down_W', 'L2_cond_down_b',
        'L2_cond_up_W', 'L2_cond_up_b', 'L2_cond_expert_W', 'L2_cond_expert_b', 'L2_cond_domain_emb',
        'L2_cond_ln_gamma', 'L2_cond_ln_beta', 'L3_cond_A_grid', 'L3_cond_B_grid']


def constants():
    import numpy as np
    own, other = [3.5, -4.5, 2.5, -0.5], [0.5, -1.5, 1.5, -0.5]
    return {
        "freqs": np.exp(np.arange(HALF, dtype=np.float32) * np.float32(-math.log(10000.0) / (HALF - 1))),
        "expert_ids": np.arange(EXPERTS, dtype=np.float32),
        "edge_weights": np.array(other + own + own[::-1] + other[::-1] + own + other, np.float32),
    }


def program(nc, a, out_dram):
    B = a["x"].shape[0]

    def scratch(name, shape):
        return nc.dram_tensor(name, shape, F32, kind="Internal").ap()

    cond_dram, bias_dram = scratch("cond_rows", [B, COND]), scratch("bias_rows", [P, D])
    x1_dram, y_dram = scratch("x1_rows", [B, S, D]), scratch("y_rows", [B, S, D])
    edge_dram, ghost_dram = scratch("edge_rows", [2, 2 * T, D]), scratch("ghost_rows", [2, D])
    setup(nc, a, cond_dram, bias_dram)
    attention(nc, a, cond_dram, bias_dram, x1_dram)
    feed_forward(nc, a, x1_dram, y_dram)
    stencil(nc, a, y_dram, edge_dram, ghost_dram, out_dram)


def kernel(**inputs):
    import numpy as np
    import concourse.bacc as bacc
    from concourse.bass_utils import run_bass_kernel_spmd

    nc = bacc.Bacc("TRN2", target_bir_lowering=False, num_devices=1)
    arrays, args = {}, {}
    given = {n: np.ascontiguousarray(inputs[n]) for n in _INS}
    for name, array in {**given, **constants()}.items():
        arrays[f"in_{name}"] = array
        args[name] = nc.dram_tensor(f"in_{name}", array.shape, mybir.dt.from_np(array.dtype), kind="ExternalInput").ap()
    out = nc.dram_tensor("out_0", given["x"].shape, F32, kind="ExternalOutput").ap()
    program(nc, args, out)
    return run_bass_kernel_spmd(nc, [arrays], core_ids=[0]).results[0]["out_0"]
```

```python
import math
from contextlib import ExitStack

import concourse.bass as bass
import concourse.mybir as mybir
from concourse.alu_op_type import AluOpType as ALU

ACT = mybir.ActivationFunctionType
F32 = mybir.dt.float32
F32R = mybir.dt.float32r
BF16 = mybir.dt.bfloat16
I32 = mybir.dt.int32
U8 = mybir.dt.uint8

P = 128
S = 512
D = 512
T = S // P
DT = D // P
HEADS = 16
DH = D // HEADS
GH = P // DH
GROUPS = HEADS // GH
STEPS = GROUPS * T
UNITS = STEPS * GH
FF = 2048
FT = FF // P
ADP = 128
EXPERTS = 16
MASKED = -1.0e30
EPS = 1e-5
HALF = D // 2
COND = 2 * D + 4

START = 1

TWO_PI_A = 6.28125
TWO_PI_B = 0.00193500518798828125
TWO_PI_C = 2 * math.pi - TWO_PI_A - TWO_PI_B
ROUND = 1.5 * 2.0 ** 23
PI_IN = 3.1415925


def apart(engine, passed):
    engine.sem_inc(passed, 1)


def identity(nc, pool, ident, zeroed):
    nc.gpsimd.memset(ident[:, :], 0.0).then_inc(zeroed, 1)
    pool.wait_ge(zeroed, 1)
    return nc.gpsimd.affine_select(out=ident[:, :], in_=ident[:, :], compare_op=ALU.not_equal, fill=1.0,
                                   base=0, pattern=[[-1, P]], channel_multiplier=1)


def setup(nc, a, cond_dram, bias_dram):
    B = a["x"].shape[0]
    with ExitStack() as ctx:
        def sb(name, shape, dt=F32):
            return ctx.enter_context(nc.sbuf_tensor("su_" + name, shape, dt))

        def sem(name):
            return ctx.enter_context(nc.semaphore("su_" + name))

        ident = sb("ident", [P, P])
        w_ada = sb("w_ada", [P, DT, 2 * D])
        wo = sb("wo", [P, DT, D])
        bv = sb("bv", [P, DT])
        bo = sb("bo", [P, D])
        b_ada = sb("b_ada", [B, 2 * D])
        freqs = sb("freqs", [B, HALF])
        step_i = sb("step_i", [B, 1], I32)
        step_x = sb("step_x", [B, 2])
        angle = sb("angle", [B, 2, HALF + 2])
        turns = sb("turns", [B, 2, HALF + 2])
        waves = sb("waves", [B, 2, HALF + 2])
        silu = sb("silu", [B, D])
        silu_t = sb("silu_t", [P, DT, B])
        cond = sb("cond", [B, COND])
        bias = sb("bias", [P, D])
        ps_t = ctx.enter_context(nc.psum_tensor("su_ps_t", [P, 512], F32))
        ps_c = ctx.enter_context(nc.psum_tensor("su_ps_c", [P, 2, 512], F32))
        ps_b = ctx.enter_context(nc.psum_tensor("su_ps_b", [P, 512], F32))
        small_in, wada_in, wo_in = sem("small_in"), sem("wada_in"), sem("wo_in")
        zeroed, ident_made, chain, waved = sem("zeroed"), sem("ident_made"), sem("chain"), sem("waved")
        turned, turned_out, cond_mm, bias_mm = sem("turned"), sem("turned_out"), sem("cond_mm"), sem("bias_mm")
        rows_done, stored = sem("rows_done"), sem("stored")
        SMALL = 7

        with nc.Block() as block:
            @block.sync
            def _(sp):
                sp.dma_start(step_i[:, :], a["itok_B_34_63"].rearrange("(b o) -> b o", o=1)).then_inc(small_in, 16)
                sp.dma_start(freqs[:, :], a["freqs"].partition_broadcast(B)).then_inc(small_in, 16)
                for c in range(2):
                    sp.dma_start(angle[:, c, HALF:HALF + 1], a["condB_theta"].rearrange("(b o) -> b o", o=1)).then_inc(small_in, 16)
                    sp.dma_start(angle[:, c, HALF + 1:HALF + 2], a["condB_phi"].rearrange("(b o) -> b o", o=1)).then_inc(small_in, 16)
                sp.dma_start(b_ada[:, :], a["L1_cond_b_ada"].partition_broadcast(B)).then_inc(small_in, 16)
                sp.dma_start(w_ada[:, :, :], a["L1_cond_W_ada"].rearrange("(t p) n -> p t n", p=P)).then_inc(wada_in, 16)
                sp.dma_start(wo[:, :, :], a["L1_cond_Wo"].rearrange("(t p) n -> p t n", p=P)).then_inc(wo_in, 16)
                sp.dma_start(bv[:, :], a["L1_cond_bv"].rearrange("(t p) -> p t", p=P), allow_slow_non_contiguous=True).then_inc(wo_in, 16)
                sp.dma_start(bo[:, :], a["L1_cond_bo"].partition_broadcast(P)).then_inc(wo_in, 16)
                sp.wait_ge(rows_done, 2)
                sp.dma_start(cond_dram, cond[:, :]).then_inc(stored, 16)
                sp.dma_start(bias_dram, bias[:, :]).then_inc(stored, 16)
                sp.wait_ge(stored, 32)

            @block.gpsimd
            def _(pool):
                identity(nc, pool, ident, zeroed).then_inc(ident_made, 1)

            @block.vector
            def _(dve):
                done = [0]

                def then(ins):
                    ins.then_inc(chain, 1)
                    done[0] += 1
                    dve.wait_ge(chain, done[0])

                v = nc.vector
                dve.wait_ge(small_in, 16 * SMALL)
                then(v.tensor_copy(step_x[:, 0:1], step_i[:, :]))
                then(v.tensor_scalar(step_x[:, 1:2], step_x[:, 0:1], 40.0, None, ALU.mult))
                for c in range(2):
                    then(v.tensor_scalar(angle[:, c, 0:HALF], freqs[:, :], step_x[:, 1:2], None, ALU.mult))
                for c in range(2):
                    then(v.tensor_scalar(turns[:, c, :], angle[:, c, :], 1 / (2 * math.pi), 0.25 * c, ALU.mult, ALU.add))
                then(v.tensor_scalar(turns[:, :, :], turns[:, :, :], ROUND, None, ALU.add))
                then(v.tensor_scalar(turns[:, :, :], turns[:, :, :], ROUND, None, ALU.subtract))
                for part in (TWO_PI_A, TWO_PI_B, TWO_PI_C):
                    then(v.scalar_tensor_tensor(angle[:, :, :], turns[:, :, :], -part, angle[:, :, :], ALU.mult, ALU.add))
                then(v.tensor_scalar(angle[:, 1, :], angle[:, 1, :], math.pi / 2, None, ALU.add))
                then(v.tensor_scalar(angle[:, :, :], angle[:, :, :], PI_IN, -PI_IN, ALU.min, ALU.max))
                dve.wait_ge(turned, 1)
                v.tensor_copy(silu_t[:, :, :].rearrange("p t b -> p (t b)"), ps_t[:, 0:DT * B]).then_inc(turned_out, 1)
                dve.wait_ge(cond_mm, 1)
                v.tensor_tensor(cond[:, 0:2 * D].rearrange("b (c n) -> b c n", c=2), ps_c[0:B, :, :],
                                b_ada[:, :].rearrange("b (c n) -> b c n", c=2), ALU.add).then_inc(chain, 1)
                dve.wait_ge(chain, done[0] + 1)
                v.tensor_scalar(cond[:, 0:D], cond[:, 0:D], 1.0, None, ALU.add).then_inc(chain, 1)
                v.tensor_copy(cond[:, 2 * D:2 * D + 4].rearrange("b (c n) -> b c n", c=2),
                              waves[:, :, HALF:HALF + 2]).then_inc(rows_done, 1)
                dve.wait_ge(bias_mm, 1)
                v.tensor_tensor(bias[:, :], ps_b[:, :], bo[:, :], ALU.add).then_inc(rows_done, 1)

            @block.scalar
            def _(act):
                act.wait_ge(chain, 13)
                nc.scalar.activation(waves[:, :, :], angle[:, :, :], ACT.Sin).then_inc(waved, 1)
                act.wait_ge(waved, 1)
                nc.scalar.activation(silu[:, :].rearrange("b (c n) -> b c n", c=2), waves[:, :, 0:HALF],
                                     ACT.Silu).then_inc(waved, 1)

            @block.tensor
            def _(pe):
                pe.wait_ge(ident_made, 1)
                pe.wait_ge(waved, 2)
                for t in range(DT):
                    last = nc.tensor.transpose(ps_t[:, t * B:(t + 1) * B], silu[:, t * P:(t + 1) * P], ident[0:B, 0:B])
                last.then_inc(turned, 1)
                pe.wait_ge(turned_out, 1)
                pe.wait_ge(wada_in, 16)
                for c in range(2):
                    for t in range(DT):
                        last = nc.tensor.matmul(ps_c[0:B, c, :], silu_t[:, t, :], w_ada[:, t, c * D:(c + 1) * D],
                                                start=(t == 0), stop=(t == DT - 1))
                last.then_inc(cond_mm, 1)
                pe.wait_ge(wo_in, 48)
                for t in range(DT):
                    last = nc.tensor.matmul(ps_b[:, :], bv[:, t:t + 1].to_broadcast([P, P]), wo[:, t, :],
                                            start=(t == 0), stop=(t == DT - 1))
                last.then_inc(bias_mm, 1)


def attention(nc, a, cond_dram, bias_dram, x1_dram):
    B = a["x"].shape[0]
    with ExitStack() as ctx:
        def sb(name, shape, dt=F32):
            return ctx.enter_context(nc.sbuf_tensor("at_" + name, shape, dt))

        def sem(name):
            return ctx.enter_context(nc.semaphore("at_" + name))

        def bank(name):
            return ctx.enter_context(nc.psum_tensor("at_" + name, [P, 512], F32))

        ident = sb("ident", [P, P])
        split = [[sb(f"{n}_{part}", [P, DT, D], F32R) for part in ("hi", "lo")] for n in ("wq", "wk", "wv")]
        wq, wk, wv = split
        wo = sb("wo", [P, DT, D])
        bq_raw, bq, bk = sb("bq_raw", [P, GROUPS]), sb("bq", [P, GROUPS]), sb("bk", [P, GROUPS])
        bo = sb("bo", [P, D])
        power, eps = sb("power", [P, T]), sb("eps", [P, T])
        x_in = sb("x_in", [P, T, D])
        cond = sb("cond", [P, COND])
        rot_a, rot_b = sb("rot_a", [P, P]), sb("rot_b", [P, P])
        stats = sb("stats", [P, T, 6])
        moments = sb("moments", [P, T, 2])
        rstd = sb("rstd", [P, T])
        xn = x_in
        residual = sb("residual", [P, T, D])
        mask_in = sb("mask_in", [P, T, S], U8)
        masked_add = sb("masked_add", [P, T, S], BF16)
        ident_bf = sb("ident_bf", [P, P], BF16)
        xt = [sb(f"xt_{part}", [P, DT, S], F32R) for part in ("hi", "lo")]
        v_sb = sb("v_sb", [P, T, D])
        q_parts = [sb(f"q_{part}", [P, S], F32R) for part in ("hi", "lo")]
        k_parts = [sb(f"k_{part}", [P, S], F32R) for part in ("hi", "lo")]
        KR = 3 * DH
        q_stack = [sb(f"q_stack{i}", [KR, GH, S], F32R) for i in range(2)]
        k_stack = [sb(f"k_stack{i}", [KR, GH, S], F32R) for i in range(2)]
        SLOTS = 4
        RING = SLOTS * GH
        passed = ctx.enter_context(nc.semaphore("at_passed"))
        probs = sb("probs", [P, RING, S])
        probs_t = [sb(f"probs_t{i}", [P, GH, T, P]) for i in range(2)]
        neg_max = [sb(f"neg_max{i}", [P, GH]) for i in range(2)]
        sums = [sb(f"sums{i}", [P, GH]) for i in range(2)]
        spoilt = [sb(f"spoilt{i}", [P, GH]) for i in range(2)]
        recip = [sb(f"recip{i}", [P, GH]) for i in range(2)]
        recip_b = [sb(f"recip_b{i}", [P, P]) for i in range(2)]
        ctx_t = sb("ctx_t", [P, GROUPS, S])

        ps_s = [bank(f"ps_s{i}") for i in range(2)]
        ps_p = [bank(f"ps_p{i}") for i in range(2)]
        ps_x = [bank(f"ps_x{i}") for i in range(2)]
        ps_m = [bank(f"ps_m{i}") for i in range(2)]

        weights_in, zeroed, ident_made, consts = sem("weights_in"), sem("zeroed"), sem("ident_made"), sem("consts")
        x_landed, cond_landed, mask_landed = sem("x_landed"), sem("cond_landed"), sem("mask_landed")
        bias_landed = [sem(f"bias_landed{i}") for i in range(SLOTS)]
        mask_made, bias_masked = sem("mask_made"), sem("bias_masked")
        norm_chain, rstd_made, xn_ready, residual_made = sem("norm_chain"), sem("rstd_made"), sem("xn_ready"), sem("residual_made")
        mod_chain = sem("mod_chain")
        rounded, weights_split = sem("rounded"), sem("weights_split")
        stacked = [sem(f"stacked{i}") for i in range(2)]
        job_filled = [sem(f"job_filled{i}") for i in range(2)]
        job_taken = [sem(f"job_taken{i}") for i in range(2)]
        scores_ready, scores_biased, probs_ready = sem("scores_ready"), sem("scores_biased"), sem("probs_ready")
        probs_turned = sem("probs_turned")
        turned_taken = [sem(f"turned_taken{i}") for i in range(2)]
        recip_made, recip_ready, recip_spread, recip_copied = sem("recip_made"), sem("recip_ready"), sem("recip_spread"), sem("recip_copied")
        spoil_chain = sem("spoil_chain")
        ctx_ready, ctx_taken, x1_made, x1_stored = sem("ctx_ready"), sem("ctx_taken"), sem("x1_made"), sem("x1_stored")

        JOB_V, JOB_X = 0, T + 2 * (GROUPS - 1)
        JOB_O = [JOB_X + DT + k for k in (0, 2, 4, 5)]
        JOB_Q0, JOB_K0 = JOB_X + DT + 1, JOB_X + DT + 3
        JOBS = T + 2 * GROUPS + DT + T
        NJ = JOBS // 2
        BEFORE = JOB_X // 2
        BEHIND = (3, 1)
        PARTS = DT + 2 * GROUPS
        PART_X, PART_Q0 = 2 * (GROUPS - 1), 2 * (GROUPS - 1) + DT
        TURN, TAKE, CONTEXT, SPREAD = 2, 3, 8, 11
        STACKS = 16 * 3 * GH
        MOD = 2 * T
        NORM = 8 * T + 3 * T

        bias_dram_tiles = a["fside_Bx16xSxS_0"].rearrange("b h (p t) k -> b h t p k", t=T)

        def job_q(g):
            return T + 2 * (g - 1)

        def filled(b, n):
            return NJ * (b + 1) + n // 2 + 1

        def slot_q(g):
            return max((g - 1) * T * GH - 3, 0)

        def slot_o(j):
            return (STEPS - T + j) * GH + SPREAD + 3

        ON_POOL = [u for g in range(1, GROUPS) for u in range(slot_q(g), slot_q(g) + 8)]
        STACK_AT = {3: [(0, 0), (0, 1)], 4: [(1, 0)], 5: [(1, 1)], 6: [(2, 0)], 7: [(2, 1)], 10: [(3, 0)], 11: [(3, 1)]}
        SLOT_X = slot_o(0) - 6
        SLOT_Q0, SLOT_K0 = slot_o(0) + 0, slot_o(1) + 1

        with nc.Block() as block:
            @block.sync
            def _(sp):
                for counted in job_taken:
                    sp.sem_inc(counted, BEFORE)
                for counted in [*job_taken, *turned_taken, *stacked, x1_stored, mod_chain, norm_chain]:
                    sp.sem_inc(counted, START)
                def next_inputs(n):
                    sp.dma_start(x_in[:, :, :], a["x"][n].rearrange("(p t) d -> p t d", t=T)).then_inc(x_landed, 16)
                    sp.dma_start(cond[:, :], cond_dram[n].partition_broadcast(P)).then_inc(cond_landed, 16)
                    sp.dma_start(mask_in[:, :, :], a["mask_Bx1xSxS_bk0"][n, 0].rearrange("(p t) k -> p t k", t=T)).then_inc(mask_landed, 16)

                def stack(b, g, which):
                    parts, out, order = ((q_parts, q_stack, (0, 0, 1)), (k_parts, k_stack, (0, 1, 0)))[which]
                    job = job_q(g) + which if g else (JOB_Q0, JOB_K0)[which]
                    sp.wait_ge(job_taken[job % 2], START + filled(b if g else b - 1, job))
                    apart(sp, passed)
                    for h in range(GH):
                        for row, part in enumerate(order):
                            sp.dma_start(out[g % 2][row * DH:(row + 1) * DH, h, :].bitcast(F32),
                                         parts[part][h * DH:(h + 1) * DH, :].bitcast(F32)).then_inc(stacked[which], 16)

                next_inputs(0)
                for w, n in ((residual, "Wq"), (ctx_t, "Wk"), (v_sb, "Wv"), (wo, "Wo")):
                    sp.dma_start(w[:, :, :], a["L1_cond_" + n].rearrange("(t p) n -> p t n", p=P)).then_inc(weights_in, 16)
                sp.dma_start(bq_raw[:, :], a["L1_cond_bq"].rearrange("(t p) -> p t", p=P), allow_slow_non_contiguous=True).then_inc(weights_in, 16)
                sp.dma_start(bk[:, :], a["L1_cond_bk"].rearrange("(t p) -> p t", p=P), allow_slow_non_contiguous=True).then_inc(weights_in, 16)
                sp.dma_start(bo[:, :], bias_dram).then_inc(weights_in, 16)

                with sp.Fori(0, B) as b:
                    following = sp.snap((b + 1) % B)
                    for s in range(STEPS):
                        sp.wait_ge(probs_turned, UNITS * b + GH * s + GH)
                        apart(sp, passed)
                        g, t, slot = s // T, s % T, s % SLOTS
                        sp.dma_start(probs[:, slot * GH:(slot + 1) * GH, :],
                                     bias_dram_tiles[b, g * GH:(g + 1) * GH, t].rearrange("h p k -> p h k")).then_inc(bias_landed[slot], 16)
                        for g, which in STACK_AT.get(s, []):
                            stack(b, g, which)
                        if s == 5:
                            sp.wait_ge(residual_made, T * b + T)
                            apart(sp, passed)
                            sp.wait_ge(mask_made, b + 1)
                            apart(sp, passed)
                            next_inputs(following)
                sp.wait_ge(x1_stored, START + 16 * B)

            @block.gpsimd
            def _(pool):
                g_ = nc.gpsimd
                identity(nc, pool, ident, zeroed).then_inc(ident_made, 1)
                g_.memset(power[:, :], -0.5).then_inc(ident_made, 1)
                g_.memset(eps[:, :], EPS).then_inc(ident_made, 1)

                def inverse_deviation(n):
                    pool.wait_ge(norm_chain, START + NORM * n + NORM - T)
                    pool.wait_ge(mod_chain, START + MOD * n)
                    g_.tensor_tensor(rstd[:, :], moments[:, :, 1], eps[:, :], ALU.add).then_inc(mod_chain, 1)
                    pool.wait_ge(mod_chain, START + MOD * n + 1)
                    g_.tensor_tensor(rstd[:, :], rstd[:, :], power[:, :], ALU.pow).then_inc(rstd_made, 1)

                def modulate(n, t):
                    if t == 0:
                        pool.wait_ge(norm_chain, START + NORM * n + NORM)
                        pool.wait_ge(rstd_made, n + 1)
                    g_.tensor_tensor(xn[:, t, :], xn[:, t, :], cond[:, 0:D], ALU.mult).then_inc(mod_chain, 1)
                    pool.wait_ge(mod_chain, START + MOD * n + 2 + 2 * t)
                    g_.tensor_tensor(xn[:, t, :], xn[:, t, :], cond[:, D:2 * D],
                                     ALU.add).then_inc(xn_ready if t == T - 1 else mod_chain, 1)

                def residual_of(b, t):
                    if t == 0:
                        pool.wait_ge(x1_stored, START + 16 * b)
                        pool.wait_ge(xn_ready, b + 1)
                    g_.tensor_tensor(residual[:, t, :], xn[:, t, :], bo[:, :], ALU.add).then_inc(residual_made, 1)

                pool.wait_ge(ident_made, 3)
                inverse_deviation(0)
                for t in range(T):
                    modulate(0, t)
                pool.wait_ge(weights_in, 16 * 7)
                pool.wait_ge(weights_split, 6)
                with pool.Fori(0, B) as b:
                    pool.wait_ge(mask_made, b + 1)
                    for k, u in enumerate(ON_POOL):
                        s = u // GH
                        pool.wait_ge(bias_landed[s % SLOTS], 16 * (STEPS // SLOTS) * b + 16 * (s // SLOTS + 1))
                        tile = probs[:, u % RING, :].rearrange("p (k t) -> p t k", t=T)
                        g_.tensor_tensor(tile, tile, masked_add[:, s % T, :].rearrange("p (t k) -> p t k", t=T),
                                         ALU.add).then_inc(bias_masked, 1)
                        if 5 <= k < 5 + T:
                            residual_of(b, k - 5)
                    inverse_deviation(b + 1)
                    for t in range(T):
                        modulate(b + 1, t)

            def norm_steps(dve, v, n):
                k = [0]

                def link(ins):
                    ins.then_inc(norm_chain, 1)
                    k[0] += 1

                def ready():
                    dve.wait_ge(norm_chain, START + NORM * n + k[0])

                x4 = x_in[:, :, :].rearrange("p t (f c) -> p t f c", c=4)
                y4 = xn[:, :, :].rearrange("p t (f c) -> p t f c", c=4)
                sin, cos = cond[:, 2 * D:2 * D + 2], cond[:, 2 * D + 2:2 * D + 4]
                dve.wait_ge(x_landed, 16 * n + 16)
                dve.wait_ge(cond_landed, 16 * n + 16)
                for t in range(T):
                    for c in range(2):
                        first, second = x4[:, t, :, 2 * c], x4[:, t, :, 2 * c + 1]
                        ready()
                        link(v.tensor_scalar(rot_a[:, :], second, sin[:, c:c + 1], None, ALU.mult))
                        link(v.tensor_scalar(rot_b[:, :], first, sin[:, c:c + 1], None, ALU.mult))
                        yield
                        ready()
                        link(v.scalar_tensor_tensor(y4[:, t, :, 2 * c], first, cos[:, c:c + 1], rot_a[:, :], ALU.mult, ALU.add))
                        link(v.scalar_tensor_tensor(y4[:, t, :, 2 * c + 1], second, cos[:, c:c + 1], rot_b[:, :], ALU.mult, ALU.subtract))
                        yield
                ready()
                for t in range(T):
                    link(v.bn_stats(stats[:, t, :], xn[:, t, :]))
                    yield
                ready()
                apart(dve, passed)
                for t in range(T):
                    link(v.bn_aggr(moments[:, t, :], stats[:, t, :]))
                for _ in range(8):
                    yield
                dve.wait_ge(rstd_made, n + 1)
                ready()
                for t in range(T):
                    link(v.tensor_scalar(xn[:, t, :], xn[:, t, :], moments[:, t, 0:1], rstd[:, t:t + 1],
                                         ALU.subtract, ALU.mult))
                    yield

            @block.vector
            def _(dve):
                v = nc.vector
                dve.sem_inc(ctx_taken, 2)
                for _ in norm_steps(dve, v, 0):
                    pass
                dve.wait_ge(weights_in, 16 * 7)
                v.tensor_scalar(bq[:, :], bq_raw[:, :], DH ** -0.5, None, ALU.mult).then_inc(consts, 1)
                v.tensor_scalar(residual[:, :, :], residual[:, :, :], DH ** -0.5, None, ALU.mult).then_inc(consts, 1)
                dve.wait_ge(ident_made, 3)
                v.tensor_copy(ident_bf[:, :], ident[:, :]).then_inc(consts, 1)
                dve.wait_ge(consts, 3)
                for k, (raw, (hi, lo)) in enumerate(zip((residual, ctx_t, v_sb), split)):
                    v.tensor_copy(hi[:, :, :], raw[:, :, :]).then_inc(weights_split, 1)
                    dve.wait_ge(weights_split, 2 * k + 1)
                    v.tensor_tensor(lo[:, :, :], raw[:, :, :], hi[:, :, :].bitcast(F32), ALU.subtract).then_inc(weights_split, 1)
                dve.wait_ge(weights_split, 6)

                def take_job(b, job, out, add=None):
                    i = job % 2
                    dve.wait_ge(job_filled[i], filled(b, job))
                    if add is not None:
                        v.tensor_tensor(out, ps_m[i][:, :], add, ALU.add).then_inc(job_taken[i], 1)
                    else:
                        v.tensor_copy(out, ps_m[i][:, :]).then_inc(job_taken[i], 1)

                def take_rest(b, job, part, hi, lo, bias=None):
                    dve.wait_ge(rounded, PARTS * b + DT + 2 + part + 1)
                    i = job % 2
                    if bias is None:
                        v.tensor_tensor(lo, ps_m[i][:, :], hi.bitcast(F32), ALU.subtract).then_inc(job_taken[i], 1)
                    else:
                        v.scalar_tensor_tensor(lo, ps_m[i][:, :], bias, hi.bitcast(F32), ALU.add,
                                               ALU.subtract).then_inc(job_taken[i], 1)
                        
                def rest_q(b, g):
                    take_rest(b, job_q(g), 2 * g - 2, q_parts[0][:, :], q_parts[1][:, :], bq[:, g:g + 1])

                def rest_k(b, g):
                    take_rest(b, job_q(g) + 1, 2 * g - 1, k_parts[0][:, :], k_parts[1][:, :], bk[:, g:g + 1])

                def rest_of_next(b, n):
                    if n < DT:
                        take_rest(b, JOB_X + n, PART_X + n, xt[0][:, n, :], xt[1][:, n, :])
                    elif n == DT:
                        take_rest(b, JOB_Q0, PART_Q0, q_parts[0][:, :], q_parts[1][:, :], bq[:, 0:1])
                    else:
                        take_rest(b, JOB_K0, PART_Q0 + 1, k_parts[0][:, :], k_parts[1][:, :], bk[:, 0:1])

                def bias_and_max(b, u):
                    s, h = u // GH, u % GH
                    dve.wait_ge(scores_ready, UNITS * b + u + 1)
                    if u in ON_POOL:
                        dve.wait_ge(bias_masked, len(ON_POOL) * b + ON_POOL.index(u) + 1)
                    else:
                        dve.wait_ge(bias_landed[s % SLOTS], 16 * (STEPS // SLOTS) * b + 16 * (s // SLOTS + 1))
                    apart(dve, passed)
                    tile = probs[:, u % RING, :].rearrange("p (k t) -> p t k", t=T)
                    v.tensor_tensor_reduce(tile, ps_s[u % 2][:, :].rearrange("p (t k) -> p t k", t=T), tile,
                                           -1.0, 3.0e38, ALU.add, ALU.min,
                                           neg_max[s % 2][:, h:h + 1]).then_inc(scores_biased, 1)

                def take_turned(b, u):
                    s, h = u // GH, u % GH
                    dve.wait_ge(probs_turned, UNITS * b + u + 1 + RING)
                    if h == 1:
                        dve.wait_ge(ctx_ready, STEPS * b + s + 1)
                    v.tensor_copy(probs_t[s % 2][:, h, :, :].rearrange("p t k -> p (t k)"),
                                  ps_p[u % 2][:, :]).then_inc(turned_taken[u % 2], 1)

                def reciprocal(b, s):
                    dve.wait_ge(probs_ready, UNITS * b + GH * (s + 1))
                    i = s % 2
                    n = 3 * (STEPS * b + s)
                    v.tensor_scalar(spoilt[i][:, :], neg_max[i][:, :], 1.0e10, None, ALU.mult).then_inc(recip_made, 1)
                    v.reciprocal(recip[i][:, :], sums[i][:, :]).then_inc(recip_made, 1)
                    dve.wait_ge(recip_made, n + 2)
                    v.scalar_tensor_tensor(spoilt[i][:, :], neg_max[i][:, :], 1.0e10, spoilt[i][:, :],
                                           ALU.mult, ALU.subtract).then_inc(recip_made, 1)
                    dve.wait_ge(recip_made, n + 3)
                    v.tensor_tensor(recip[i][:, :], recip[i][:, :], spoilt[i][:, :], ALU.add).then_inc(recip_ready, 1)

                def take_ctx(b, s):
                    g, t = s // T, s % T
                    dve.wait_ge(recip_copied, STEPS * b + s + 1)
                    v.tensor_tensor(ctx_t[:, g, t * P:(t + 1) * P], ps_x[s % 2][:, 0:P], recip_b[s % 2][:, :],
                                    ALU.mult).then_inc(ctx_taken, 1)

                def make_mask(n):
                    dve.wait_ge(mask_landed, 16 * n + 16)
                    v.tensor_scalar(masked_add[:, :, :].rearrange("p q (t k) -> p q t k", t=T),
                                    mask_in[:, :, :].rearrange("p q (k t) -> p q t k", t=T), MASKED, None,
                                    ALU.mult).then_inc(mask_made, 1)

                make_mask(0)
                for n in range(DT + 2):
                    rest_of_next(-1, n)
                for i in range(2):
                    dve.wait_ge(job_taken[i], START + NJ - BEHIND[i])
                    dve.sem_inc(job_taken[i], BEHIND[i])
                with dve.Fori(0, B) as b:
                    for t in (1, 3):
                        take_job(b, JOB_V + t, v_sb[:, t, :])
                    norm = None
                    for t in range(slot_o(T - 1) + 2):
                        if 0 <= t - TAKE < UNITS and (t - TAKE) % GH == 1:
                            take_turned(b, t - TAKE)
                        if t < UNITS:
                            bias_and_max(b, t)
                        if t - 3 >= 0 and t - 3 < UNITS and (t - 3) % GH == GH - 1:
                            reciprocal(b, (t - 3) // GH)
                        for g in range(1, GROUPS):
                            if t == slot_q(g) + 4:
                                rest_q(b, g)
                            if t == slot_q(g) + 8:
                                rest_k(b, g)
                        if t >= SPREAD + 1 and (t - SPREAD - 1) % GH == 0 and (t - SPREAD - 1) // GH < STEPS:
                            take_ctx(b, (t - SPREAD - 1) // GH)
                        if t == 18:
                            norm = norm_steps(dve, v, b + 1)
                        if norm:
                            next(norm, None)
                            if t % 4 == 2:
                                next(norm, None)
                        if t == UNITS:
                            dve.wait_ge(scores_ready, UNITS * b + UNITS)
                            dve.wait_ge(bias_masked, len(ON_POOL) * b + len(ON_POOL))
                            make_mask(b + 1)
                        for n, slot in enumerate([*range(SLOT_X, SLOT_X + DT), SLOT_Q0 + 3, SLOT_K0 + 3]):
                            if t == slot + 1:
                                rest_of_next(b, n)
                        for j in range(T):
                            if t == slot_o(j) + 1:
                                dve.wait_ge(residual_made, T * b + T)
                                take_job(b, JOB_O[j], residual[:, j, :], add=residual[:, j, :])

            @block.scalar
            def _(act):
                def take_job(b, job, out):
                    i = job % 2
                    act.wait_ge(job_filled[i], filled(b, job))
                    nc.scalar.copy(out, ps_m[i][:, :]).then_inc(job_taken[i], 1)

                def round_job(b, job, out, bias=0.0):
                    i = job % 2
                    act.wait_ge(job_filled[i], filled(b, job))
                    nc.scalar.activation(out, ps_m[i][:, :], ACT.Identity, bias=bias).then_inc(rounded, 1)

                def round_q(b, g):
                    act.wait_ge(stacked[0], START + STACKS * (GROUPS * b + g))
                    round_job(b, job_q(g), q_parts[0][:, :], bq[:, g:g + 1])

                def round_k(b, g):
                    act.wait_ge(stacked[1], START + STACKS * (GROUPS * b + g))
                    round_job(b, job_q(g) + 1, k_parts[0][:, :], bk[:, g:g + 1])

                def round_next(b, n):
                    if n < DT:
                        round_job(b, JOB_X + n, xt[0][:, n, :])
                    elif n == DT:
                        act.wait_ge(stacked[0], START + STACKS * GROUPS * (b + 1))
                        round_job(b, JOB_Q0, q_parts[0][:, :], bq[:, 0:1])
                    else:
                        act.wait_ge(stacked[1], START + STACKS * GROUPS * (b + 1))
                        round_job(b, JOB_K0, k_parts[0][:, :], bk[:, 0:1])

                def exponent(b, u):
                    s, h = u // GH, u % GH
                    act.wait_ge(scores_biased, UNITS * b + u + 1)
                    tile = probs[:, u % RING, :]
                    nc.scalar.activation(tile, tile, ACT.Exp, scale=-1.0, bias=neg_max[s % 2][:, h:h + 1],
                                         accum_out=sums[s % 2][:, h:h + 1]).then_inc(probs_ready, 1)

                def take_turned(b, u):
                    s, h = u // GH, u % GH
                    act.wait_ge(probs_turned, UNITS * b + u + 1 + RING)
                    if h == 0:
                        act.wait_ge(ctx_ready, STEPS * b + s + 1)
                    nc.scalar.copy(probs_t[s % 2][:, h, :, :].rearrange("p t k -> p (t k)"),
                                   ps_p[u % 2][:, :]).then_inc(turned_taken[u % 2], 1)

                def copy_recip(b, s):
                    act.wait_ge(recip_spread, STEPS * b + s + 1)
                    act.wait_ge(ctx_taken, STEPS * b + s + 1)
                    nc.scalar.copy(recip_b[s % 2][:, :], ps_x[s % 2][:, P:2 * P]).then_inc(recip_copied, 1)

                act.wait_ge(consts, 1)
                for n in range(DT + 2):
                    round_next(-1, n)
                with act.Fori(0, B) as b:
                    for t in (0, 2):
                        take_job(b, JOB_V + t, v_sb[:, t, :])
                    for t in range(slot_o(T - 1) + 1):
                        if 0 <= t - TAKE < UNITS and (t - TAKE) % GH != 1:
                            take_turned(b, t - TAKE)
                        if t < UNITS:
                            exponent(b, t)
                        for g in range(1, GROUPS):
                            if t == slot_q(g) + 4:
                                round_q(b, g)
                            if t == slot_q(g) + 8:
                                round_k(b, g)
                        for n, slot in enumerate([*range(SLOT_X, SLOT_X + DT), SLOT_Q0 + 3, SLOT_K0 + 3]):
                            if t == slot + 1:
                                round_next(b, n)
                        if t >= SPREAD + 1 and (t - SPREAD - 1) % GH == 0 and (t - SPREAD - 1) // GH < STEPS:
                            copy_recip(b, (t - SPREAD - 1) // GH)
                    for i in range(2):
                        act.wait_ge(job_taken[i], START + NJ * (b + 1) + NJ)
                    act.dma_start(x1_dram[b].rearrange("(p t) d -> p t d", t=T), residual[:, :, :]).then_inc(x1_stored, 16)

            @block.tensor
            def _(pe):
                def job(b, n, products, quarters=range(4)):
                    i = n % 2
                    if quarters[0] == 0:
                        pe.wait_ge(job_taken[i], START + NJ * (b + 1) + n // 2)
                    share = len(products) // 4
                    for k in range(share * quarters[0], share * (quarters[-1] + 1)):
                        lhs, rhs = products[k]
                        last = nc.tensor.matmul(ps_m[i][:, :], lhs, rhs, start=(k == 0), stop=(k == len(products) - 1))
                    if quarters[-1] == 3:
                        last.then_inc(job_filled[i], 1)

                def parts(left, l_at, right, r_at):
                    return [(left[i][l_at], right[j][r_at]) for i, j in ((0, 0), (0, 1), (1, 0))]

                def project(b, w, n, g, quarters=range(4)):
                    cols = slice(g * P, (g + 1) * P)
                    job(b, n, [pair for t in range(DT)
                               for pair in parts(w, (slice(None), t, cols), xt, (slice(None), t, slice(None)))],
                        quarters)

                def scores(b, u):
                    s, h = u // GH, u % GH
                    g, t = s // T, s % T
                    if u == 0:
                        pe.wait_ge(mask_made, b + 1)
                    if s % T == 0 and h == 0:
                        for i in range(2):
                            pe.wait_ge(stacked[i], START + STACKS * (GROUPS * b + g + 1))
                    if u >= 2:
                        pe.wait_ge(scores_biased, UNITS * b + u - 1)
                    product = nc.tensor.matmul(ps_s[u % 2][:, :], q_stack[g % 2][:, h, t * P:(t + 1) * P],
                                               k_stack[g % 2][:, h, :], start=True, stop=u in ON_POOL)
                    if u in ON_POOL:
                        product.then_inc(scores_ready, 1)
                        return
                    nc.tensor.matmul(ps_s[u % 2][:, :], ident_bf[:, :], masked_add[:, t, :],
                                     start=False, stop=True).then_inc(scores_ready, 1)

                def turn(b, u):
                    s, h = u // GH, u % GH
                    pe.wait_ge(probs_ready, UNITS * b + u + 1)
                    pe.wait_ge(turned_taken[u % 2], START + (UNITS // 2) * b + u // 2)
                    for t in range(T):
                        last = nc.tensor.transpose(ps_p[u % 2][:, t * P:(t + 1) * P],
                                                   probs[:, u % RING, t:S:T], ident[:, :])
                    last.then_inc(probs_turned, 1)

                def context(b, s, t):
                    g = s // T
                    if t == 0:
                        for i in range(2):
                            pe.wait_ge(turned_taken[i], START + (UNITS // 2) * b + 2 * s + 2)
                        pe.wait_ge(ctx_taken, STEPS * b + s + 1)
                    for h in range(GH):
                        col = g * P + h * DH
                        last = nc.tensor.matmul(ps_x[s % 2][h * DH:(h + 1) * DH, 0:P], v_sb[:, t, col:col + DH],
                                                probs_t[s % 2][:, h, t, :], start=(t == 0), stop=(t == T - 1))
                    if t < T - 1:
                        return
                    last.then_inc(ctx_ready, 1)
                    pe.wait_ge(recip_ready, STEPS * b + s + 1)
                    for h in range(GH):
                        last = nc.tensor.matmul(ps_x[s % 2][h * DH:(h + 1) * DH, P:2 * P],
                                                recip[s % 2][:, h:h + 1].to_broadcast([P, DH]), ident[:, :],
                                                start=True, stop=True)
                    last.then_inc(recip_spread, 1)

                def turn_x(b, t):
                    i = t % 2
                    if t == 0:
                        pe.wait_ge(xn_ready, b + 2)
                    pe.wait_ge(job_taken[i], START + NJ * (b + 1) + (JOB_X + t) // 2)
                    for j in range(T):
                        last = nc.tensor.transpose(ps_m[i][:, j * P:(j + 1) * P], xn[:, j, t * P:(t + 1) * P], ident[:, :])
                    last.then_inc(job_filled[i], 1)

                def first_group(b, which, quarters=range(4)):
                    if which == 0 and quarters[0] == 0:
                        for i in range(2):
                            pe.wait_ge(job_taken[i], START + NJ * (b + 1) + (JOB_X + DT) // 2)
                    project(b, (wq, wk)[which], (JOB_Q0, JOB_K0)[which], 0, quarters)

                pe.wait_ge(weights_in, 16 * 7)
                pe.wait_ge(weights_split, 6)
                pe.wait_ge(ident_made, 3)
                pe.wait_ge(consts, 3)
                pe.sem_inc(probs_turned, RING)
                pe.sem_inc(ctx_ready, 2)
                for i in range(2):
                    pe.sem_inc(job_filled[i], BEFORE)
                for t in range(DT):
                    turn_x(-1, t)
                first_group(-1, 0)
                first_group(-1, 1)
                for i in range(2):
                    pe.wait_ge(job_filled[i], NJ - BEHIND[i])
                    pe.sem_inc(job_filled[i], BEHIND[i])
                with pe.Fori(0, B) as b:
                    for j in range(T):
                        job(b, JOB_V + j, [pair for t in range(DT)
                                           for pair in parts(xt, (slice(None), t, slice(j * P, (j + 1) * P)),
                                                             wv, (slice(None), t, slice(None)))])
                    for t in range(slot_o(T - 1) + 1):
                        if t < UNITS:
                            scores(b, t)
                        if 0 <= t - TURN < UNITS:
                            turn(b, t - TURN)
                        s, part = (t - CONTEXT) // GH, (t - CONTEXT) % GH
                        if 0 <= s < STEPS:
                            context(b, s, part)
                        for g in range(1, GROUPS):
                            part = t - slot_q(g)
                            if 0 <= part < 4:
                                project(b, wq, job_q(g), g, [part])
                            if 4 <= part < 8:
                                project(b, wk, job_q(g) + 1, g, [part - 4])
                        if SLOT_X <= t < SLOT_X + DT:
                            turn_x(b, t - SLOT_X)
                        for which, slot in enumerate((SLOT_Q0, SLOT_K0)):
                            if 0 <= t - slot < 4:
                                first_group(b, which, [t - slot])
                        for j in range(T):
                            if t == slot_o(j):
                                pe.wait_ge(ctx_taken, STEPS * b + STEPS - T + j + 1 + 2)
                                job(b, JOB_O[j], [(ctx_t[:, g, j * P:(j + 1) * P], wo[:, g, :]) for g in range(GROUPS)])


def feed_forward(nc, a, x1_dram, edge_dram, ghost_dram, out_dram):
    B = a["x"].shape[0]
    with ExitStack() as ctx:
        def sb(name, shape, dt=F32):
            return ctx.enter_context(nc.sbuf_tensor("ff_" + name, shape, dt))

        def sem(name):
            return ctx.enter_context(nc.semaphore("ff_" + name))

        def bank(name):
            return ctx.enter_context(nc.psum_tensor("ff_" + name, [P, 512], F32))

        ident = sb("ident", [P, P])
        w1, w2 = sb("w1", [P, DT, FF]), sb("w2", [P, FT, D])
        b1 = sb("b1", [P, FT])
        b2, g2, beta2 = sb("b2", [P, D]), sb("g2", [P, DT]), sb("beta2", [P, DT])
        down_t, down_b = sb("down_t", [P, DT, ADP]), sb("down_b", [P, 1])
        up_t, up_b = sb("up_t", [P, D]), sb("up_b", [P, D])
        experts_t = sb("experts_t", [P, EXPERTS, ADP])
        gamma, beta = sb("gamma", [P, D]), sb("beta", [P, D])
        ids, id_col = sb("ids", [P, EXPERTS]), sb("id_col", [EXPERTS, 1])
        expert_b, expert_e = sb("expert_b", [EXPERTS, ADP]), sb("expert_e", [EXPERTS, ADP])
        dom_i, dom, dom_in = sb("dom_i", [P, B], I32), sb("dom", [P, B]), sb("dom_in", [P, B])
        valid = sb("valid", [P, B])
        pick = sb("pick", [P, B, EXPERTS + 1])
        pick_e, pick_b = sb("pick_e", [EXPERTS, B]), sb("pick_b", [EXPERTS, B])
        shift_all = sb("shift_all", [P, B])
        pick_now, shift_now = sb("pick_now", [P, EXPERTS + 1]), sb("shift_now", [P, 1])
        expert = [sb(f"expert{i}", [P, ADP]) for i in range(2)]
        power, eps = sb("power", [P, T]), sb("eps", [P, T])
        x1 = sb("x1", [P, T, D])
        hidden = x1
        stats, moments, rstd = sb("stats", [P, T, 6]), sb("moments", [P, T, 2]), sb("rstd", [P, T])
        ht = sb("ht", [P, DT, S])
        RING = 4
        act_t = sb("act_t", [P, RING, S])
        x2 = sb("x2", [P, T, D])
        x2t = sb("x2t", [P, DT, S])
        low = sb("low", [P, S])
        mixed = low
        y = x2
        down, up = act_t[:, 0, :], act_t[:, 1, :].rearrange("p (t n) -> p t n", t=DT)
        experts = x2t[:, :, :].rearrange("p t d -> p (t d)").rearrange("p (e i) -> p e i", e=EXPERTS)
        stats_y, moments_y, rstd_y = sb("stats_y", [P, T, 6]), sb("moments_y", [P, T, 2]), sb("rstd_y", [P, T])
        ps = [bank(f"ps{i}") for i in range(4)]
        acc = [bank(f"acc{i}") for i in range(T)]

        W = D + 2
        edges = sb("edges", [P, 3, 2 * T])
        dts, dt_now = sb("dts", [P, B + 1]), sb("dt_now", [P, 1])
        f = sb("f", [P, T, D])
        q = sb("q", [P, T, W])
        w = sb("w", [P, T, D])
        v0 = sb("v0", [P, T, D])
        v1 = sb("v1", [P, T, D])
        row_up, row_dn = sb("row_up", [P, T + 1, D]), sb("row_dn", [P, T + 1, D])
        cols = sb("cols", [P, T, 2, W])
        total = q[:, :, 1:D + 1]
        chunk = 2 * D // P
        near = sb("near", [P, 2 * T, chunk])
        ghost = sb("ghost", [P, chunk])
        col_p = sb("col_p", [P, T, 2, T])

        weights_in, zeroed, ident_made = sem("weights_in"), sem("zeroed"), sem("ident_made")
        pick_chain, picked, consts = sem("pick_chain"), sem("picked"), sem("consts")
        setup_mm, setup_taken = sem("setup_mm"), sem("setup_taken")
        x1_landed, norm_chain, rstd_made, hidden_ready = sem("x1_landed"), sem("norm_chain"), sem("rstd_made"), sem("hidden_ready")
        filled = [sem(f"filled{i}") for i in range(4)]
        taken = [sem(f"taken{i}") for i in range(4)]
        x1_base, expert_chain = sem("x1_base"), sem("expert_chain")
        x2_base, y_chain, rstd_y_made, y_ready = sem("x2_base"), sem("y_chain"), sem("rstd_y_made"), sem("y_ready")
        passed = sem("passed")
        eps_chain, gamma_done = sem("eps_chain"), sem("gamma_done")
        x2_landed, act_used, acc_filled, acc_taken = sem("x2_landed"), sem("act_used"), sem("acc_filled"), sem("acc_taken")
        w1_in = [sem(f"w1_in{i}") for i in range(4)]
        w2_in = [sem(f"w2_in{i}") for i in range(4)]
        small_in, q_in, row_grids_in, col_grids_in = sem("small_in"), sem("q_in"), sem("row_grids_in"), sem("col_grids_in")
        rows_made, rows_out, near_in = sem("rows_made"), sem("rows_out"), sem("near_in")
        ghost_made, ghost_out, rows_in, shifted = sem("ghost_made"), sem("ghost_out"), sem("rows_in"), sem("shifted")
        cols_made, neighbours_made, batch_done, stored = sem("cols_made"), sem("neighbours_made"), sem("batch_done"), sem("stored")
        dve_chain, edge_cols = sem("dve_chain"), sem("edge_cols")
        LINKS = 20

        EARLY = 3
        JOB_1 = [0] * FT
        JOB_1[EARLY:] = range(FT - EARLY)
        JOB_H = FT - EARLY
        JOB_X = JOB_H + DT
        JOB_1[0], JOB_DOWN, JOB_1[1], JOB_MIX, JOB_1[2] = range(JOB_X + DT, JOB_X + DT + 5)
        JOB_UP = JOB_1[2] + 1
        JOBS = JOB_UP + T
        JOBS += -JOBS % 4
        NJ = JOBS // 4
        EMPTY = range(JOB_UP + T, JOBS)

        def count(b, job):
            return NJ * (b + 1) + job // 4 + 1

        NORM = 3 * T
        Y_NORM = 3 * T
        WEIGHTS = 14

        with nc.Block() as block:
            @block.sync
            def _(sp):
                for counted in [*taken, acc_taken, x2_base, stored, dve_chain, batch_done]:
                    sp.sem_inc(counted, START)
                def load(out, array, **how):
                    sp.dma_start(out, array, **how).then_inc(weights_in, 16)

                def by_rows(array):
                    return array.rearrange("(p t) d -> p t d", t=T)

                sp.dma_start(x1[:, :, :], by_rows(x1_dram[0])).then_inc(x1_landed, 16)
                load(down, a["L2_cond_down_W"])
                load(up, a["L2_cond_up_W"].rearrange("(t p) n -> p t n", p=P))
                load(experts, a["L2_cond_expert_W"].rearrange("e o i -> o e i"))
                load(dom_i[:, :], a["itok_B_0_15"].partition_broadcast(P))
                load(ids[:, :], a["expert_ids"].partition_broadcast(P))
                load(id_col[:, :], a["expert_ids"].rearrange("(e o) -> e o", o=1))
                load(expert_b[:, :], a["L2_cond_expert_b"])
                load(expert_e[:, :], a["L2_cond_domain_emb"])
                for out, n in ((b1, "L1_cond_b1"), (g2, "L1_cond_g2"), (beta2, "L1_cond_beta2"), (down_b, "L2_cond_down_b")):
                    load(out[:, :], a[n].rearrange("(t p) -> p t", p=P), allow_slow_non_contiguous=True)
                for out, n in ((b2, "L1_cond_b2"), (up_b, "L2_cond_up_b")):
                    load(out[:, :], a[n].partition_broadcast(P))
                for i in range(4):
                    part, n = slice(i * FF // 4, (i + 1) * FF // 4), FT // 4
                    sp.dma_start(w1[:, :, part], a["L1_cond_W1"][:, part].rearrange("(t p) n -> p t n", p=P)).then_inc(w1_in[i], 16)
                    sp.dma_start(w2[:, i * n:(i + 1) * n, :], a["L1_cond_W2"][part].rearrange("(t p) n -> p t n", p=P)).then_inc(w2_in[i], 16)
                sp.dma_start(gamma[:, :], a["L2_cond_ln_gamma"].partition_broadcast(P)).then_inc(consts, 16)
                sp.dma_start(beta[:, :], a["L2_cond_ln_beta"].partition_broadcast(P)).then_inc(consts, 16)
                sp.dma_start(edges[:, :, :].rearrange("p a b -> p (a b)"), a["edge_weights"].partition_broadcast(P)).then_inc(small_in, 16)
                sp.dma_start(dts[:, 1:B + 1], a["condB_dt"].partition_broadcast(P)).then_inc(small_in, 16)

                def load_grids(n):
                    sp.wait_ge(stored, START + 16 * n)
                    apart(sp, passed)
                    sp.dma_start(q[:, :, 1:D + 1], by_rows(a["L3_cond_B_grid"][2])).then_inc(q_in, 16)
                    sp.dma_start(w[:, :, :], by_rows(a["L3_cond_A_grid"][0])).then_inc(row_grids_in, 16)
                    sp.dma_start(v0[:, :, :], by_rows(a["L3_cond_B_grid"][0])).then_inc(row_grids_in, 16)
                    sp.dma_start(cols[:, :, 0, 1:D + 1], by_rows(a["L3_cond_A_grid"][1])).then_inc(col_grids_in, 16)
                    sp.dma_start(v1[:, :, :], by_rows(a["L3_cond_B_grid"][1])).then_inc(col_grids_in, 16)

                def outer_rows(n):
                    sp.wait_ge(rows_made, n + 1)
                    sp.dma_start(row_up[0:P - 1, T, :], row_up[1:P, 0, :]).then_inc(shifted, 16)
                    sp.dma_start(row_dn[1:P, 0, :], row_dn[0:P - 1, T, :]).then_inc(shifted, 16)
                    sp.dma_start(edge_dram[0, 0:T], row_dn[0:1, 1:T + 1, :]).then_inc(rows_out, 16)
                    sp.dma_start(edge_dram[0, T:2 * T], row_up[0:1, 0:T, :]).then_inc(rows_out, 16)
                    for t in range(T):
                        sp.dma_start(edge_dram[1, t:t + 1], row_up[P - 1:P, T - 1 - t:T - t, :]).then_inc(rows_out, 16)
                        sp.dma_start(edge_dram[1, T + t:T + t + 1], row_dn[P - 1:P, T - t:T - t + 1, :]).then_inc(rows_out, 16)
                    sp.wait_ge(rows_out, 160 * n + 160)
                    for k in range(2):
                        sp.dma_start(near[k * P // 2:(k + 1) * P // 2, :, :],
                                     edge_dram[k].rearrange("r (c i) -> c r i", i=chunk)).then_inc(near_in, 16)
                    sp.wait_ge(ghost_made, n + 1)
                    sp.dma_start(ghost_dram.rearrange("k (c i) -> (k c) i", i=chunk), ghost[:, :]).then_inc(ghost_out, 16)
                    sp.wait_ge(ghost_out, 16 * n + 16)
                    sp.dma_start(row_dn[0:1, 0, :], ghost_dram[0:1]).then_inc(rows_in, 16)
                    sp.dma_start(row_up[P - 1:P, T, :], ghost_dram[1:2]).then_inc(rows_in, 16)

                def store(n, batch):
                    sp.wait_ge(batch_done, START + n + 1)
                    apart(sp, passed)
                    sp.dma_start(by_rows(out_dram[batch]), total).then_inc(stored, 16)

                with sp.Fori(0, B) as b:
                    following = sp.snap((b + 1) % B)
                    before = sp.snap((b + B - 1) % B)
                    load_grids(b)
                    sp.wait_ge(y_ready, b + 1)
                    apart(sp, passed)
                    sp.dma_start(x2[:, :, :], by_rows(x1_dram[b])).then_inc(x2_landed, 16)
                    for i in range(4):
                        sp.wait_ge(filled[(JOB_H + i) % 4], count(b - 1, JOB_H + i))
                        apart(sp, passed)
                    sp.dma_start(x1[:, :, :], by_rows(x1_dram[following])).then_inc(x1_landed, 16)
                    outer_rows(b)
                    store(b, before)
                load_grids(B)
                outer_rows(B)
                store(B, B - 1)
                sp.wait_ge(stored, START + 16 * (B + 1))
                sp.wait_ge(x1_landed, 16 * B + 16)

            @block.gpsimd
            def _(pool):
                g_ = nc.gpsimd
                identity(nc, pool, ident, zeroed).then_inc(ident_made, 1)
                g_.memset(eps[:, :], EPS).then_inc(ident_made, 1)
                g_.memset(dts[:, 0:1], 0.0).then_inc(ident_made, 1)
                pool.wait_ge(ident_made, 3)
                g_.memset(power[:, :], -0.5).then_inc(eps_chain, 1)
                g_.memset(f[:, :, :], 0.0).then_inc(y_ready, 1)

                def inverse_deviation(n, out, source, ready, chain_before, made):
                    pool.wait_ge(ready, chain_before)
                    pool.wait_ge(eps_chain, n)
                    g_.tensor_tensor(out[:, :], source[:, :, 1], eps[:, :], ALU.add).then_inc(eps_chain, 1)
                    pool.wait_ge(eps_chain, n + 1)
                    g_.tensor_tensor(out[:, :], out[:, :], power[:, :], ALU.pow).then_inc(made, 1)

                def base_of_x2(b):
                    pool.wait_ge(x2_landed, 16 * b + 16)
                    g_.tensor_tensor(x2[:, :, :], x2[:, :, :], b2[:, :].unsqueeze(1).to_broadcast([P, T, D]),
                                     ALU.add).then_inc(x1_base, 1)

                def stencil_columns(n):
                    c0, c1 = cols[:, :, 0, 1:D + 1], cols[:, :, 1, 1:D + 1]
                    pool.wait_ge(col_grids_in, 32 * n + 32)
                    pool.wait_ge(y_ready, n + 1)
                    g_.tensor_tensor(v1[:, :, :], v1[:, :, :], f[:, :, :], ALU.mult).then_inc(cols_made, 1)
                    g_.tensor_tensor(c0, c0, f[:, :, :], ALU.mult).then_inc(cols_made, 1)
                    pool.wait_ge(cols_made, 6 * n + 2)
                    pool.wait_ge(batch_done, START + n)
                    g_.tensor_tensor(c1, v1[:, :, :], c0, ALU.add).then_inc(cols_made, 1)
                    pool.wait_ge(cols_made, 6 * n + 3)
                    g_.tensor_tensor(c0, v1[:, :, :], c0, ALU.subtract).then_inc(cols_made, 1)
                    pool.wait_ge(cols_made, 6 * n + 4)
                    pool.wait_ge(rows_made, n + 1)
                    g_.tensor_tensor(v1[:, :, :], v0[:, :, :], v1[:, :, :], ALU.add).then_inc(cols_made, 1)
                    pool.wait_ge(cols_made, 6 * n + 5)
                    pool.wait_ge(edge_cols, 2 * n + 2)
                    g_.tensor_tensor(v0[:, :, :], cols[:, :, 0, 2:W], cols[:, :, 1, 0:D], ALU.add).then_inc(cols_made, 1)

                pool.wait_ge(weights_in, 16 * WEIGHTS)
                inverse_deviation(1, rstd, moments, norm_chain, 2 * T, rstd_made)
                with pool.Fori(0, B) as b:
                    base_of_x2(b)
                    inverse_deviation(2 * b + 2, rstd, moments, norm_chain, NORM * b + NORM + 2 * T, rstd_made)
                    stencil_columns(b)
                    pool.wait_ge(filled[(JOB_X + DT - 1) % 4], count(b, JOB_X + DT - 1))
                    g_.tensor_tensor(x2[:, :, :], x2[:, :, :], up_b[:, :].unsqueeze(1).to_broadcast([P, T, D]),
                                     ALU.add).then_inc(x2_base, 1)
                    inverse_deviation(2 * b + 3, rstd_y, moments_y, y_chain, Y_NORM * b + 2 * T, rstd_y_made)
                stencil_columns(B)

            def statistics(dve, v, source, stats, moments, chain, base):
                for t in range(T):
                    v.bn_stats(stats[:, t, :], source[:, t, :]).then_inc(chain, 1)
                dve.wait_ge(chain, base + T)
                apart(dve, passed)
                for t in range(T):
                    v.bn_aggr(moments[:, t, :], stats[:, t, :]).then_inc(chain, 1)

            def normalise(dve, v, out, source, moments, rstd, chain):
                for t in range(T):
                    v.tensor_scalar(out[:, t, :], source[:, t, :], moments[:, t, 0:1], rstd[:, t:t + 1],
                                    ALU.subtract, ALU.mult).then_inc(chain, 1)

            @block.vector
            def _(dve):
                v = nc.vector
                done = [0]

                def then(ins):
                    ins.then_inc(pick_chain, 1)
                    done[0] += 1
                    dve.wait_ge(pick_chain, done[0])

                dve.wait_ge(weights_in, 16 * WEIGHTS)
                dve.wait_ge(ident_made, 3)
                then(v.tensor_copy(dom_in[:, :], dom_i[:, :]))
                then(v.tensor_scalar(dom[:, :], dom_in[:, :], 0.0, float(EXPERTS - 1), ALU.max, ALU.min))
                then(v.tensor_tensor(valid[:, :], dom[:, :], dom_in[:, :], ALU.is_equal))
                for n in range(B):
                    then(v.tensor_scalar(pick[:, n, 0:EXPERTS], ids[:, :], dom[:, n:n + 1], valid[:, n:n + 1],
                                         ALU.is_equal, ALU.mult))
                then(v.tensor_scalar(pick[:, :, EXPERTS], valid[:, :], -1.0, 1.0, ALU.mult, ALU.add))
                then(v.tensor_scalar(pick_e[:, :], dom[0:EXPERTS, :], id_col[:, :], None, ALU.is_equal))
                then(v.tensor_tensor(pick_b[:, :], pick_e[:, :], valid[0:EXPERTS, :], ALU.mult))
                v.memset(low[:, 0:1], 0.0).then_inc(picked, 1)
                for k in range(6):
                    out = [down_t[:, :, :], up_t[:, :].rearrange("p (t n) -> p t n", t=DT)] + \
                          [experts_t[:, 4 * i:4 * i + 4, :] for i in range(4)]
                    dve.wait_ge(setup_mm, k + 1)
                    v.tensor_copy(out[k], ps[k % 4][:, :].rearrange("p (t n) -> p t n", t=4)).then_inc(setup_taken, 1)
                dve.wait_ge(setup_mm, 7)
                v.tensor_copy(shift_all[:, :], ps[2][:, 0:B]).then_inc(setup_taken, 1)
                dve.wait_ge(setup_taken, 7)

                def skip(b, jobs):
                    for job in jobs:
                        dve.wait_ge(filled[job % 4], count(b, job))
                        dve.sem_inc(taken[job % 4], 1)

                skip(-1, range(JOB_H))
                dve.wait_ge(x1_landed, 16)
                statistics(dve, v, x1, stats, moments, norm_chain, 0)
                dve.wait_ge(rstd_made, 1)
                normalise(dve, v, hidden, x1, moments, rstd, norm_chain)

                def stencil_rows(n, column):
                    k = [0]

                    def link(ins):
                        ins.then_inc(dve_chain, 1)
                        k[0] += 1

                    def ready():
                        dve.wait_ge(dve_chain, START + LINKS * n + k[0])

                    inner = q[:, :, 1:D + 1]
                    dve.wait_ge(y_ready, n + 1)
                    dve.wait_ge(q_in, 16 * n + 16)
                    ready()
                    link(v.tensor_scalar(dt_now[:, :], dts[:, column], 0.5, None, ALU.mult))
                    link(v.tensor_tensor(inner, inner, f[:, :, :], ALU.mult))
                    ready()
                    for out, x0, x1_, x2_ in ((0, 1, 2, 3), (D + 1, D, D - 1, D - 2)):
                        link(v.tensor_tensor(q[:, :, out], q[:, :, x0], q[:, :, x1_], ALU.subtract))
                        ready()
                        link(v.scalar_tensor_tensor(q[:, :, out], q[:, :, out], 3.0, q[:, :, x2_], ALU.mult, ALU.add))
                        ready()
                    slope = row_up[:, 0:T, :]
                    link(v.tensor_tensor(slope, q[:, :, 2:W], q[:, :, 0:D], ALU.subtract))
                    dve.wait_ge(row_grids_in, 32 * n + 32)
                    link(v.tensor_tensor(w[:, :, :], w[:, :, :], f[:, :, :], ALU.mult))
                    link(v.tensor_tensor(v0[:, :, :], v0[:, :, :], f[:, :, :], ALU.mult))
                    ready()
                    link(v.scalar_tensor_tensor(w[:, :, :], slope, -0.5, w[:, :, :], ALU.mult, ALU.add))
                    ready()
                    link(v.tensor_tensor(row_up[:, 0:T, :], v0[:, :, :], w[:, :, :], ALU.subtract))
                    link(v.tensor_tensor(row_dn[:, 1:T + 1, :], v0[:, :, :], w[:, :, :], ALU.add))
                    ready()
                    v.sem_inc(rows_made, 1)
                    dve.wait_ge(cols_made, 6 * n + 4)
                    for c, (out, first) in enumerate(((0, 1), (D + 1, D + 1 - T))):
                        link(v.tensor_tensor(col_p[:, :, :, :], cols[:, :, :, first:first + T],
                                             edges[:, c, :].rearrange("p (a k) -> p a k", a=2).unsqueeze(1).to_broadcast([P, T, 2, T]),
                                             ALU.mult))
                        ready()
                        v.tensor_reduce(cols[:, :, 1 - c, out], col_p[:, :, :, :], mybir.AxisListType.XY,
                                        ALU.add).then_inc(edge_cols, 1)
                        dve.wait_ge(edge_cols, 2 * n + c + 1)
                    dve.wait_ge(near_in, 32 * n + 32)
                    link(v.tensor_tensor(near[:, :, :], near[:, :, :],
                                         edges[:, 2, :].unsqueeze(2).to_broadcast([P, 2 * T, chunk]), ALU.mult))
                    ready()
                    v.tensor_reduce(ghost[:, :], near[:, :, :].rearrange("p r i -> p i r"), mybir.AxisListType.X,
                                    ALU.add).then_inc(ghost_made, 1)
                    dve.wait_ge(shifted, 32 * n + 32)
                    dve.wait_ge(rows_in, 32 * n + 32)
                    link(v.tensor_tensor(total, row_up[:, 1:T + 1, :], row_dn[:, 0:T, :], ALU.add))
                    ready()
                    dve.wait_ge(cols_made, 6 * n + 6)
                    link(v.scalar_tensor_tensor(total, v1[:, :, :], -2.0, total, ALU.mult, ALU.add))
                    ready()
                    link(v.tensor_tensor(total, total, v0[:, :, :], ALU.add))
                    ready()
                    link(v.scalar_tensor_tensor(total, total, dt_now[:, :], f[:, :, :], ALU.mult, ALU.add))
                    ready()
                    v.tensor_scalar(total, total, 0.0, None, ALU.max).then_inc(batch_done, 1)
                    dve.wait_ge(batch_done, START + n + 1)
                    dve.sem_inc(dve_chain, 1)
                    assert k[0] + 1 == LINKS, k[0]

                skip(-1, [*range(JOB_X, JOB_X + DT), JOB_DOWN, JOB_MIX, *range(JOB_UP, JOBS)])
                dve.wait_ge(small_in, 32)
                dve.wait_ge(consts, 32)
                with dve.Fori(0, B) as b:
                    def take(job):
                        dve.wait_ge(filled[job % 4], count(b, job))
                        return ps[job % 4][:, :]

                    E = (EXPERTS + 3) * b
                    v.tensor_copy(pick_now[:, :], pick[:, bass.ds(b, 1), :].rearrange("p o e -> p (o e)")).then_inc(expert_chain, 1)
                    v.tensor_copy(shift_now[:, :], shift_all[:, bass.ds(b, 1)]).then_inc(expert_chain, 1)
                    dve.wait_ge(expert_chain, E + 2)
                    v.tensor_scalar(expert[0][:, :], ident[:, :], pick_now[:, EXPERTS:EXPERTS + 1], None,
                                    ALU.mult).then_inc(expert_chain, 1)
                    for e in range(EXPERTS):
                        dve.wait_ge(expert_chain, E + 3 + e)
                        v.scalar_tensor_tensor(expert[(e + 1) % 2][:, :], experts_t[:, e, :], pick_now[:, e:e + 1],
                                               expert[e % 2][:, :], ALU.mult, ALU.add).then_inc(expert_chain, 1)
                    dve.wait_ge(x1_landed, 16 * b + 32)
                    statistics(dve, v, x1, stats, moments, norm_chain, NORM * b + NORM)
                    dve.wait_ge(rstd_made, b + 2)
                    normalise(dve, v, hidden, x1, moments, rstd, norm_chain)
                    stencil_rows(b, bass.ds(b, 1))
                    dve.wait_ge(x1_base, b + 1)
                    for t in range(T):
                        dve.wait_ge(acc_filled, T * b + t + 1)
                        v.tensor_tensor(x2[:, t, :], acc[t][:, :], x2[:, t, :], ALU.add).then_inc(acc_taken, 1)
                    for t in range(1, DT, 2):
                        v.tensor_copy(x2t[:, t, :], take(JOB_X + t)).then_inc(taken[(JOB_X + t) % 4], 1)
                    v.tensor_scalar(mixed[:, :], take(JOB_MIX), shift_now[:, :], None, ALU.add).then_inc(taken[JOB_MIX % 4], 1)
                    dve.wait_ge(x2_base, START + b + 1)
                    for t in range(T):
                        v.tensor_tensor(y[:, t, :], take(JOB_UP + t), x2[:, t, :], ALU.add).then_inc(taken[(JOB_UP + t) % 4], 1)
                    for t in range(T):
                        dve.wait_ge(taken[(JOB_UP + t) % 4], START + count(b, JOB_UP + t))
                    skip(b, EMPTY)
                    statistics(dve, v, y, stats_y, moments_y, y_chain, Y_NORM * b)
                    dve.wait_ge(rstd_y_made, b + 1)
                    normalise(dve, v, y, y, moments_y, rstd_y, y_chain)
                    dve.wait_ge(y_chain, Y_NORM * b + Y_NORM)
                    v.tensor_tensor(y[:, :, :], y[:, :, :], gamma[:, :].unsqueeze(1).to_broadcast([P, T, D]),
                                    ALU.mult).then_inc(gamma_done, 1)
                    dve.wait_ge(gamma_done, b + 1)
                    v.tensor_tensor(f[:, :, :], y[:, :, :], beta[:, :].unsqueeze(1).to_broadcast([P, T, D]),
                                    ALU.add).then_inc(y_ready, 1)
                stencil_rows(B, slice(B, B + 1))

            @block.scalar
            def _(act):
                act.wait_ge(weights_in, 16 * WEIGHTS)

                def take(b, job):
                    act.wait_ge(filled[job % 4], count(b, job))
                    return ps[job % 4][:, :]

                def turned(b):
                    for t in range(DT):
                        nc.scalar.activation(ht[:, t, :], take(b, JOB_H + t), ACT.Identity, scale=g2[:, t:t + 1],
                                             bias=beta2[:, t:t + 1]).then_inc(taken[(JOB_H + t) % 4], 1)

                def activated(b, n, k):
                    act.wait_ge(act_used, FT * n + k + 1)
                    nc.scalar.activation(act_t[:, k % RING, :], take(b, JOB_1[k]), ACT.Gelu_apprx_sigmoid,
                                         bias=b1[:, k:k + 1]).then_inc(taken[JOB_1[k] % 4], 1)

                turned(-1)
                for k in range(EARLY):
                    activated(-1, 0, k)
                with act.Fori(0, B) as b:
                    for k in range(EARLY, FT):
                        activated(b, b, k)
                    turned(b)
                    for t in range(0, DT, 2):
                        nc.scalar.copy(x2t[:, t, :], take(b, JOB_X + t)).then_inc(taken[(JOB_X + t) % 4], 1)
                    activated(b, b + 1, 0)
                    nc.scalar.activation(low[:, :], take(b, JOB_DOWN), ACT.Gelu,
                                         bias=down_b[:, 0:1]).then_inc(taken[JOB_DOWN % 4], 1)
                    activated(b, b + 1, 1)
                    activated(b, b + 1, 2)

            @block.tensor
            def _(pe):
                pe.wait_ge(weights_in, 16 * WEIGHTS)
                pe.wait_ge(ident_made, 1)
                for k in range(6):
                    if k >= 4:
                        pe.wait_ge(setup_taken, k - 3)
                    for i in range(4):
                        source = down[:, i * P:(i + 1) * P] if k == 0 else up[:, i, :] if k == 1 else experts[:, 4 * (k - 2) + i, :]
                        last = nc.tensor.transpose(ps[k % 4][:, i * P:(i + 1) * P], source, ident[:, :])
                    last.then_inc(setup_mm, 1)
                pe.wait_ge(picked, 1)
                pe.wait_ge(setup_taken, 3)
                nc.tensor.matmul(ps[2][:, 0:B], expert_b[:, :], pick_b[:, :], start=True, stop=False)
                nc.tensor.matmul(ps[2][:, 0:B], expert_e[:, :], pick_e[:, :], start=False, stop=True).then_inc(setup_mm, 1)
                pe.wait_ge(setup_taken, 7)
                pe.sem_inc(act_used, RING)

                def free(b, job):
                    pe.wait_ge(taken[job % 4], START + count(b, job) - 1)

                def until_taken(b, job, n):
                    for k in range(max(job, job + n - 4), job + n):
                        pe.wait_ge(taken[k % 4], START + count(b, k))

                def product(b, job, pairs):
                    free(b, job)
                    for k, (lhs, rhs) in enumerate(pairs):
                        last = nc.tensor.matmul(ps[job % 4][:, :], lhs, rhs, start=(k == 0), stop=(k == len(pairs) - 1))
                    last.then_inc(filled[job % 4], 1)

                def first_product(b, k):
                    pe.wait_ge(w1_in[k * 4 // FT], 16)
                    product(b, JOB_1[k], [(w1[:, t, k * P:(k + 1) * P], ht[:, t, :]) for t in range(DT)])

                def turn(b, job, source):
                    for t in range(DT):
                        free(b, job + t)
                        for j in range(T):
                            last = nc.tensor.transpose(ps[(job + t) % 4][:, j * P:(j + 1) * P],
                                                       source[:, j, t * P:(t + 1) * P], ident[:, :])
                        last.then_inc(filled[(job + t) % 4], 1)

                def skip(b, jobs):
                    for job in jobs:
                        free(b, job)
                        pe.sem_inc(filled[job % 4], 1)

                skip(-1, range(JOB_H))
                pe.wait_ge(norm_chain, NORM)
                turn(-1, JOB_H, hidden)
                skip(-1, range(JOB_X, JOB_X + DT))
                until_taken(-1, JOB_H, DT)
                first_product(-1, 0)
                skip(-1, [JOB_DOWN])
                first_product(-1, 1)
                skip(-1, [JOB_MIX])
                first_product(-1, 2)
                skip(-1, range(JOB_UP, JOBS))
                with pe.Fori(0, B) as b:
                    for i in range(FT):
                        if i + EARLY < FT:
                            first_product(b, i + EARLY)
                        pe.wait_ge(w2_in[i * 4 // FT], 16)
                        until_taken(b - 1 if i < EARLY else b, JOB_1[i], 1)
                        if i == 0:
                            pe.wait_ge(acc_taken, START + T * b)
                        for j in range(T):
                            last = nc.tensor.matmul(acc[j][:, :], act_t[:, i % RING, j * P:(j + 1) * P], w2[:, i, :],
                                                    start=(i == 0), stop=(i == FT - 1))
                            if i == FT - 1:
                                last.then_inc(acc_filled, 1)
                        if i < FT - 1:
                            last.then_inc(act_used, 1)
                    pe.wait_ge(norm_chain, NORM * (b + 1) + NORM)
                    turn(b, JOB_H, hidden)
                    pe.wait_ge(acc_filled, T * b + T)
                    pe.sem_inc(act_used, 1)
                    pe.wait_ge(acc_taken, START + T * b + T)
                    turn(b, JOB_X, x2)
                    until_taken(b, JOB_H, DT)
                    first_product(b, 0)
                    until_taken(b, JOB_X, DT)
                    product(b, JOB_DOWN, [(down_t[:, t, :], x2t[:, t, :]) for t in range(DT)])
                    first_product(b, 1)
                    until_taken(b, JOB_DOWN, 1)
                    pe.wait_ge(expert_chain, (EXPERTS + 3) * b + EXPERTS + 3)
                    product(b, JOB_MIX, [(expert[EXPERTS % 2][:, :], low[:, :])])
                    first_product(b, 2)
                    until_taken(b, JOB_MIX, 1)
                    for j in range(T):
                        product(b, JOB_UP + j, [(mixed[:, j * P:(j + 1) * P], up_t[:, :])])
                    skip(b, EMPTY)


_INS = ['x', 'condB_theta', 'condB_phi', 'itok_B_34_63', 'fside_Bx16xSxS_0', 'itok_B_0_15', 'condB_dt',
        'mask_Bx1xSxS_bk0', 'L1_cond_W_ada', 'L1_cond_b_ada', 'L1_cond_Wq', 'L1_cond_bq', 'L1_cond_Wk',
        'L1_cond_bk', 'L1_cond_Wv', 'L1_cond_bv', 'L1_cond_Wo', 'L1_cond_bo', 'L1_cond_W1', 'L1_cond_b1',
        'L1_cond_W2', 'L1_cond_b2', 'L1_cond_g2', 'L1_cond_beta2', 'L2_cond_down_W', 'L2_cond_down_b',
        'L2_cond_up_W', 'L2_cond_up_b', 'L2_cond_expert_W', 'L2_cond_expert_b', 'L2_cond_domain_emb',
        'L2_cond_ln_gamma', 'L2_cond_ln_beta', 'L3_cond_A_grid', 'L3_cond_B_grid']


def constants():
    import numpy as np
    own, other = [3.5, -4.5, 2.5, -0.5], [0.5, -1.5, 1.5, -0.5]
    return {
        "freqs": np.exp(np.arange(HALF, dtype=np.float32) * np.float32(-math.log(10000.0) / (HALF - 1))),
        "expert_ids": np.arange(EXPERTS, dtype=np.float32),
        "edge_weights": np.array(other + own + own[::-1] + other[::-1] + own + other, np.float32),
    }


def program(nc, a, out_dram):
    B = a["x"].shape[0]

    def scratch(name, shape):
        return nc.dram_tensor(name, shape, F32, kind="Internal").ap()

    cond_dram, bias_dram = scratch("cond_rows", [B, COND]), scratch("bias_rows", [P, D])
    x1_dram = scratch("x1_rows", [B, S, D])
    edge_dram, ghost_dram = scratch("edge_rows", [2, 2 * T, D]), scratch("ghost_rows", [2, D])
    setup(nc, a, cond_dram, bias_dram)
    attention(nc, a, cond_dram, bias_dram, x1_dram)
    feed_forward(nc, a, x1_dram, edge_dram, ghost_dram, out_dram)


def kernel(**inputs):
    import numpy as np
    import concourse.bacc as bacc
    from concourse.bass_utils import run_bass_kernel_spmd

    nc = bacc.Bacc("TRN2", target_bir_lowering=False, num_devices=1)
    arrays, args = {}, {}
    given = {n: np.ascontiguousarray(inputs[n]) for n in _INS}
    for name, array in {**given, **constants()}.items():
        arrays[f"in_{name}"] = array
        args[name] = nc.dram_tensor(f"in_{name}", array.shape, mybir.dt.from_np(array.dtype), kind="ExternalInput").ap()
    out = nc.dram_tensor("out_0", given["x"].shape, F32, kind="ExternalOutput").ap()
    program(nc, args, out)
    return run_bass_kernel_spmd(nc, [arrays], core_ids=[0]).results[0]["out_0"]
```
